# Optimizing a Trainium2 kernel written in Bass

```python
import numpy as np
import jax
import jax.numpy as jnp

def _softmax(x, axis=-1):
    return jax.nn.softmax(x, axis=axis)

def _gelu(x):
    return jax.nn.gelu(x, approximate=True)

def _silu(x):
    return jax.nn.silu(x)

def _sigmoid(x):
    return jax.nn.sigmoid(x)

def _layernorm(x, axis=-1, eps=1e-05):
    m = jnp.mean(x, axis=axis, keepdims=True)
    v = jnp.var(x, axis=axis, keepdims=True)
    return (x - m) / jnp.sqrt(v + eps)

def _scatter_add(tgt, idx, src, axis=0):
    return tgt.at[idx].add(src)

def _segment_sum(src, seg, n):
    return jax.ops.segment_sum(src, seg, n)
kernel_name = 'mk_xattn_ffn_d1_seqx_r8_ead616'

def setup_inputs(seed: int=0):
    np.random.seed(seed)
    _w = jnp.asarray

    def _rec_inputs():
        import jax
        import jax.numpy as jnp
        _rk = jax.random.key(seed)
        x = -0.000125 + 0.9999 * jax.random.normal(jax.random.fold_in(_rk, 1), (4, 256, 256), jnp.float32)
        _lenS = 256 - jax.random.randint(jax.random.fold_in(_rk, 7), (4,), 0, max(1, 256 // 4) + 1, jnp.int32)
        _lenS2 = 256 - jax.random.randint(jax.random.fold_in(_rk, 8), (4,), 0, max(1, 256 // 4) + 1, jnp.int32)
        itok_BxS_13_99985 = jax.random.randint(jax.random.fold_in(_rk, 11), (4, 256), 13, 99986, jnp.int32)
        _ctx_2048P = jax.random.normal(jax.random.fold_in(_rk, 12), (4, 16, 256), jnp.float32)
        _ctx_2048c = jax.random.dirichlet(jax.random.fold_in(_rk, 512), 0.3 * jnp.ones((16,), jnp.float32), (4, 256))
        _ctx_2048t = jnp.einsum('bsk,bkd->bsd', _ctx_2048c, _ctx_2048P)
        _ctx_2048t = _ctx_2048t * jax.lax.rsqrt(jnp.mean(jnp.square(_ctx_2048t)) + 1e-12) * 0.953939
        ctx_2048 = 6.82029e-06 + 0.0200006 * (_ctx_2048t + 0.3 * jax.random.normal(jax.random.fold_in(_rk, 612), (4, 256, 256), jnp.float32))
        return (x, itok_BxS_13_99985, ctx_2048)
    x, itok_BxS_13_99985, ctx_2048 = _rec_inputs()

    def _L0_xattn_setup():
        import jax, jax.numpy as jnp
        import numpy as np
        B, S, D = (4, 512, 256)
        E = 4
        F = 1024 // E
        VOCAB = 12500
        key = jax.random.key(seed)
        k1, k2, k3, k4, k5 = jax.random.split(key, 5)
        hidden_states = jax.random.normal(k1, (B, S, D), dtype=jnp.float32)
        token_ids = jax.random.randint(k2, (B, S), 0, VOCAB, dtype=jnp.int64)
        Wg = jax.random.normal(k3, (E, F, D), dtype=jnp.float32) * 0.02
        Wu = jax.random.normal(k4, (E, F, D), dtype=jnp.float32) * 0.02
        Wd = jax.random.normal(k5, (E, D, F), dtype=jnp.float32) * 0.02
        return {'hidden_states': hidden_states, 'token_ids': token_ids, 'Wg': Wg, 'Wu': Wu, 'Wd': Wd}
    _L0_xattn_all = _L0_xattn_setup()
    _L0_xattn_in = {k: v for k, v in _L0_xattn_all.items() if k in ()}
    del _L0_xattn_all

    def _L0_ffn_setup():
        import jax, jax.numpy as jnp
        import numpy as np
        TOP_K = 2
        ROUTE_SCALE = 1.0
        key = jax.random.key(seed)
        ks = jax.random.split(key, 8)
        B, S, D = (4, 256, 256)
        E, I = (8, 176)
        SI = 2 * I
        s = lambda d: 1.0 / np.sqrt(d)
        return {'x': jax.random.normal(ks[0], (B, S, D), jnp.float32), 'gate_w': jax.random.normal(ks[1], (E, D), jnp.float32) * s(D), 'w1': jax.random.normal(ks[2], (E, I, D), jnp.float32) * s(D), 'w2': jax.random.normal(ks[3], (E, D, I), jnp.float32) * s(I), 'w3': jax.random.normal(ks[4], (E, I, D), jnp.float32) * s(D), 'sw1': jax.random.normal(ks[5], (SI, D), jnp.float32) * s(D), 'sw2': jax.random.normal(ks[6], (D, SI), jnp.float32) * s(SI), 'sw3': jax.random.normal(ks[7], (SI, D), jnp.float32) * s(D)}
    _L0_ffn_all = _L0_ffn_setup()
    _L0_ffn_in = {k: v for k, v in _L0_ffn_all.items() if k in ('gate_w', 'w1', 'w2', 'w3', 'sw1', 'sw2', 'sw3')}
    del _L0_ffn_all
    return {'x': x, 'itok_BxS_13_99985': itok_BxS_13_99985, 'ctx_2048': ctx_2048, 'L0_ffn_gate_w': _L0_ffn_in['gate_w'], 'L0_ffn_w1': _L0_ffn_in['w1'], 'L0_ffn_w2': _L0_ffn_in['w2'], 'L0_ffn_w3': _L0_ffn_in['w3'], 'L0_ffn_sw1': _L0_ffn_in['sw1'], 'L0_ffn_sw2': _L0_ffn_in['sw2'], 'L0_ffn_sw3': _L0_ffn_in['sw3']}

def reference(x, itok_BxS_13_99985, ctx_2048, L0_ffn_gate_w, L0_ffn_w1, L0_ffn_w2, L0_ffn_w3, L0_ffn_sw1, L0_ffn_sw2, L0_ffn_sw3):
    import jax
    import jax.numpy as jnp

    def _L0_xattn_ref(hidden_states, token_ids, Wg, Wu, Wd):
        import jax, jax.numpy as jnp
        import numpy as np
        B, S, D = (4, 512, 256)
        E = 4
        F = 1024 // E
        VOCAB = 12500
        tokens_per_expert = VOCAB // E
        tid = jnp.clip(token_ids, 0, VOCAB - 1)
        expert_ids = jnp.minimum(tid // tokens_per_expert, E - 1)
        out = jnp.zeros_like(hidden_states)
        for e in range(E):
            g = jax.nn.silu(jnp.einsum('bsd,fd->bsf', hidden_states, Wg[e]))
            u = jnp.einsum('bsd,fd->bsf', hidden_states, Wu[e])
            y = jnp.einsum('bsf,df->bsd', g * u, Wd[e])
            out = jnp.where((expert_ids == e)[..., None], y, out)
        return out

    def _L0_ffn_ref(x, gate_w, w1, w2, w3, sw1, sw2, sw3):
        import jax, jax.numpy as jnp
        import numpy as np
        TOP_K = 2
        ROUTE_SCALE = 1.0
        B, S, D = x.shape
        E = gate_w.shape[0]
        xt = x.reshape(-1, D)
        T = xt.shape[0]
        scores = jax.nn.softmax((xt @ gate_w.T).astype(jnp.float32), axis=-1)
        top_w, top_idx = jax.lax.top_k(scores, TOP_K)
        top_w = (top_w * ROUTE_SCALE).astype(x.dtype)
        dense_w = jnp.zeros((T, E), x.dtype).at[jnp.arange(T)[:, None], top_idx].add(top_w)
        y = jnp.zeros_like(xt)
        for e in range(E):
            h = jax.nn.silu(xt @ w1[e].T) * (xt @ w3[e].T)
            y = y + dense_w[:, e:e + 1] * (h @ w2[e].T)
        z = jax.nn.silu(xt @ sw1.T) * (xt @ sw3.T) @ sw2.T
        return (y + z).reshape(B, S, D)
    x = x + _L0_xattn_ref(_layernorm(x, axis=-1), itok_BxS_13_99985, ctx_2048, ctx_2048, ctx_2048)
    x = x + _L0_ffn_ref(_layernorm(x, axis=-1), L0_ffn_gate_w, L0_ffn_w1, L0_ffn_w2, L0_ffn_w3, L0_ffn_sw1, L0_ffn_sw2, L0_ffn_sw3)
    return x

_drawn_inputs = setup_inputs


def setup_inputs(seed=0):
    import zlib

    import numpy as np

    out = dict(_drawn_inputs(seed))
    spreads = {}
    factors = {}
    for name, (base, spread) in spreads.items():
        noise = np.random.default_rng([zlib.crc32(name.encode()), seed]).standard_normal(out[name].shape)
        drawn = base * np.exp(spread * noise) if base else spread * noise
        out[name] = jnp.asarray(drawn.astype(out[name].dtype))
    for name, factor in factors.items():
        out[name] = (out[name] * factor).astype(out[name].dtype)
    return out
```

```python
from contextlib import ExitStack

import concourse.bass as bass
from concourse import mybir

P = 128
T, D = 1024, 256
KD = D // P
HALVES = 2
TH = T // HALVES
TT = TH // P
EA = 4
FA = 256
IDS_PER_EXPERT = 12500 // EA
EB, IB = 8, 176
SHARED = 2 * IB
SHARED_TILES = -(-SHARED // P)
ROUTED_TILES = EB * IB // P
TILES_B = SHARED_TILES + ROUTED_TILES
WCOLS = 2 * KD * P + D
EPS = 1e-5
E_FLOAT = 2.718281828459045

TILES_A = EA * FA // P
STEPS_A = HALVES * TILES_A
STEPS_B = HALVES * TILES_B
STEPS = STEPS_A + STEPS_B
LAG_A = 2
RAW = 4
TOP = 2

AT_LN1_STATS, AT_LN1_NORM, AT_LN1_TURN = 0, 2, 4
AT_LN2A_STATS, AT_LN2A_NORM, AT_LN2A_TURN, AT_GATE_A, AT_ROUTE_A = 9, 10, 12, 13, 14
B0 = STEPS_A
AT_DENSE_A = B0 + 1
AT_LN2B_STATS, AT_LN2B_NORM, AT_LN2B_TURN, AT_GATE_B, AT_ROUTE_B = B0 + 1, B0 + 2, B0 + 5, B0 + 7, B0 + 8
AT_DENSE_B = B0 + 11
AT_OUT_A = B0 + TILES_B + 1

F32 = mybir.dt.float32
F32R = mybir.dt.float32r
I32 = mybir.dt.int32
U32 = mybir.dt.uint32
ALU = mybir.AluOpType
ACT = mybir.ActivationFunctionType
AX_X = mybir.AxisListType.X


def build(nc, x, tok, ctx_t, gate_t, w_b, consts, sel, out):
    x_tiles = x.rearrange("(t p) d -> p t d", p=P)
    out_tiles = out.rearrange("(t p) d -> p t d", p=P)

    with ExitStack() as ctx:
        def sb(name, shape, dt=F32):
            return ctx.enter_context(nc.sbuf_tensor(name, shape, dt))

        def bank(name):
            return ctx.enter_context(nc.psum_tensor(name, [P, 512], F32))

        def sem(name):
            return ctx.enter_context(nc.semaphore(name))

        xt = sb("xt", [P, HALVES * TT, D])
        ids = sb("ids", [P, T])
        cst = sb("cst", [P, P + TT * EB])
        ident = cst[:, 0:P]
        iota = cst[:, P:P + TT * EB].rearrange("p (t e) -> p t e", t=TT)
        sel_r = sb("sel_r", [P, ROUTED_TILES * P], F32R)
        c_raw = sb("c_raw", [P, EA, KD * D])
        c_hi = sb("c_hi", [P, EA, KD * D], F32R)
        c_lo = sb("c_lo", [P, EA, KD * D], F32R)
        w_raw = sb("w_raw", [P, RAW, WCOLS])
        w_hi = sb("w_hi", [P, TILES_B, WCOLS], F32R)
        w_lo = sb("w_lo", [P, TILES_B, WCOLS], F32R)
        sel_raw = w_raw[:, 0:2, :].rearrange("p a n -> p (a n)")[:, 0:ROUTED_TILES * P]
        g_raw = sb("g_raw", [P, KD, EB])
        g_hl = sb("g_hl", [P, KD, 2 * EB], F32R)
        stat = sb("stat", [P, TT, 6])
        mv = sb("mv", [P, TT, 2])
        var_eps = sb("var_eps", [P, TT])
        rstd = sb("rstd", [P, TT])
        power = sb("power", [P, TT])
        base_e = sb("base_e", [P, TT, EB])
        hn = sb("hn", [P, TT, D])
        ht_hi = [sb(f"ht_hi{s}", [P, KD, T], F32R) for s in range(2)]
        ht_lo = [sb(f"ht_lo{s}", [P, KD, T], F32R) for s in range(2)]
        tm = sb("tm", [P, 2, TH])
        sg = sb("sg", [P, 2, TH])
        hb = sb("hb", [P, 2, TH])
        ids_raw = hb[:, :, :].rearrange("p a n -> p (a n)").bitcast(I32)
        h_hi = [sb(f"h_hi{s}", [P, TH], F32R) for s in range(3)]
        h_lo = [sb(f"h_lo{s}", [P, TH], F32R) for s in range(3)]
        logit = sb("logit", [P, TT, EB])
        lmax = sb("lmax", [P, TT])
        lsub = sb("lsub", [P, TT, EB])
        lexp = sb("lexp", [P, TT, EB])
        lsum = sb("lsum", [P, TT])
        lrec = sb("lrec", [P, TT])
        score = sb("score", [P, TT, EB])
        top_w = sb("top_w", [P, TT, 8])
        top_i = sb("top_i", [P, TT, 8], U32)
        top_if = sb("top_if", [P, TT, TOP])
        hit = sb("hit", [P, TOP, TT, EB])
        part = sb("part", [P, TOP, TT, EB])
        dense = sb("dense", [P, TT, EB])
        dense_hl = sb("dense_hl", [P, TT, P])
        dense_r = sb("dense_r", [P, TT, EB], F32R)
        dense_t = [sb(f"dense_t{h}", [P, TH], F32R) for h in range(HALVES)]

        work = [bank(f"work{b}") for b in range(4)]
        acc = [bank(f"acc{b}") for b in range(4)]

        x_in = [sem(f"x_in{h}") for h in range(HALVES)]
        ids_in, cst_in, sel_in, g_in = sem("ids_in"), sem("cst_in"), sem("sel_in"), sem("g_in")
        c_in = [sem(f"c_in{e}") for e in range(EA)]
        w_in = [sem(f"w_in{s}") for s in range(RAW)]
        out_done = sem("out_done")
        fills = sem("fills")
        resid = sem("resid")
        stats, moments, vars_ready = sem("stats"), sem("moments"), sem("vars_ready")
        rstds, normed = sem("rstds"), sem("normed")
        turned = sem("turned")
        ht_his, ht_los = sem("ht_his"), sem("ht_los")
        ids_step, ids_ready = sem("ids_step"), sem("ids_ready")
        c_his, c_los, w_his, w_los = sem("c_his"), sem("c_los"), sem("w_his"), sem("w_los")
        sel_ready, g_his, g_los = sem("sel_ready"), sem("g_his"), sem("g_los")
        up_a = sem("up_a")
        up_b = sem("up_b")
        spread = sem("spread")
        masked = sem("masked")
        weighted = sem("weighted")
        silus, hiddens = sem("silus"), sem("hiddens")
        hid_his, hid_los = sem("hid_his"), sem("hid_los")
        downs = sem("downs")
        gated = sem("gated")
        route = sem("route")
        shifted, exps = sem("shifted"), sem("exps")
        dense_ready, dense_turned, dense_copied = sem("dense_ready"), sem("dense_turned"), sem("dense_copied")
        summed = sem("summed")

        block = ctx.enter_context(nc.Block())

        def half_a(n):
            return n // TILES_A

        def half_b(n):
            return (n - B0) // TILES_B

        def tile_b(n):
            return (n - B0) % TILES_B

        def routed(n):
            return n >= B0 and tile_b(n) >= SHARED_TILES

        def routed_before(n):
            return sum(routed(m) for m in range(B0, n))

        def f32(ap):
            return ap.bitcast(F32)

        @block.sync
        def _(sp):
            sp.dma_start(xt[:, 0:TT, :], x_tiles[:, 0:TT, :]).then_inc(x_in[0], 16)
            sp.dma_start(c_raw[:, 0, :], ctx_t[0]).then_inc(c_in[0], 16)
            sp.dma_start(xt[:, TT:2 * TT, :], x_tiles[:, TT:2 * TT, :]).then_inc(x_in[1], 16)
            for e in range(1, EA):
                sp.dma_start(c_raw[:, e, :], ctx_t[e]).then_inc(c_in[e], 16)
            sp.dma_start(sel_raw, sel).then_inc(sel_in, 16)
            for g in range(TILES_B):
                if g == 0:
                    sp.wait_ge(sel_ready, 1)
                if g >= RAW:
                    sp.wait_ge(w_los, g - RAW + 1)
                sp.dma_start(w_raw[:, g % RAW, :], w_b[g]).then_inc(w_in[g % RAW], 16)
            for h in range(HALVES):
                for b in range(2):
                    sp.wait_ge(summed, 2 * h + b + 1)
                    sp.dma_start(out_tiles[:, TT * h + 2 * b:TT * h + 2 * b + 2, :],
                                 xt[:, TT * h + 2 * b:TT * h + 2 * b + 2, :]).then_inc(out_done, 16)
            sp.wait_ge(out_done, 16 * 2 * HALVES)

        @block.gpsimd
        def _(pool):
            pool.memset(power[:, :], -0.5).then_inc(fills, 1)
            pool.memset(base_e[:, :, :], E_FLOAT).then_inc(fills, 1)
            pool.memset(dense_hl[:, :, :], 0.0).then_inc(fills, 1)
            pool.wait_ge(fills, 3)

            def rsqrt(n):
                pool.wait_ge(vars_ready, n + 1)
                if n >= 1:
                    pool.wait_ge(normed, TT * n)
                pool.tensor_tensor(rstd[:, :], var_eps[:, :], power[:, :], ALU.pow).then_inc(rstds, 1)

            def exponent(h):
                pool.wait_ge(shifted, h + 1)
                pool.tensor_tensor(lexp[:, :, :], base_e[:, :, :], lsub[:, :, :], ALU.pow).then_inc(exps, 1)

            rsqrt(0)
            for e in range(EA):
                pool.wait_ge(c_his, e + 1)
                pool.tensor_tensor(c_lo[:, e, :], c_raw[:, e, :], f32(c_hi[:, e, :]),
                                   ALU.subtract).then_inc(c_los, 1)
            rsqrt(1)
            for g in range(TILES_B):
                pool.wait_ge(w_his, g + 1)
                pool.tensor_tensor(w_lo[:, g, :], w_raw[:, g % RAW, :], f32(w_hi[:, g, :]),
                                   ALU.subtract).then_inc(w_los, 1)
                if g == AT_LN2A_STATS - 1:
                    rsqrt(2)
            exponent(0)
            rsqrt(3)
            exponent(1)

        @block.scalar
        def _(act):
            act.dma_start(cst[:, :], consts).then_inc(cst_in, 16)
            act.dma_start(ids_raw, tok.partition_broadcast(P)).then_inc(ids_in, 16)
            act.dma_start(g_raw[:, :, :], gate_t).then_inc(g_in, 16)
            nc.scalar.preload_act_table(ACT.Silu)

            def ctx_hi(e):
                act.wait_ge(c_in[e], 16)
                act.activation(c_hi[:, e, :], c_raw[:, e, :], ACT.Copy).then_inc(c_his, 1)

            def turn_hi(n, k, src):
                s, h = n // 2, n % 2
                act.wait_ge(turned, KD * n + k + 1)
                act.activation(ht_hi[s][:, k, TH * h:TH * h + TH], src[:, :], ACT.Copy).then_inc(ht_his, 1)

            def dense_copy(h):
                act.wait_ge(dense_turned, h + 1)
                act.activation(dense_t[h][:, :], work[3][:, :], ACT.Copy).then_inc(dense_copied, 1)

            ctx_hi(0)
            for k in range(KD):
                turn_hi(0, k, work[2 + k])
            for e in range(1, EA):
                ctx_hi(e)
            act.wait_ge(sel_in, 16)
            act.activation(sel_r[:, :], sel_raw, ACT.Copy).then_inc(sel_ready, 1)
            for n in range(STEPS):
                if n < B0:
                    act.wait_ge(masked, n + 1)
                    src = tm[:, n % 2, :]
                else:
                    act.wait_ge(up_a, n + 1)
                    src = work[0][:, :]
                if n >= 2:
                    act.wait_ge(hiddens, n - 1)
                act.activation(sg[:, n % 2, :], src, ACT.Silu).then_inc(silus, 1)
                act.wait_ge(hiddens, n + 1)
                if n >= 3:
                    act.wait_ge(downs, n - 2)
                act.activation(h_hi[n % 3][:, :], hb[:, n % 2, :], ACT.Copy).then_inc(hid_his, 1)
                if 1 <= n <= TILES_B:
                    g = n - 1
                    act.wait_ge(w_in[g % RAW], 16 * (g // RAW + 1))
                    act.activation(w_hi[:, g, :], w_raw[:, g % RAW, :], ACT.Copy).then_inc(w_his, 1)
                if n == AT_LN1_TURN:
                    for k in range(KD):
                        turn_hi(1, k, work[2 + k])
                if n == AT_LN2A_TURN:
                    for k in range(KD):
                        turn_hi(2, k, work[2 + k])
                for k in range(KD):
                    if n == AT_LN2B_TURN + k:
                        turn_hi(3, k, work[3])
                if n == AT_DENSE_A:
                    dense_copy(0)
                if n == AT_DENSE_B:
                    dense_copy(1)

        @block.vector
        def _(dve):
            def norm_stats(n):
                h = n % 2
                if n < 2:
                    dve.wait_ge(x_in[h], 16)
                else:
                    dve.wait_ge(downs, TILES_A * (h + 1))
                    for b in range(2):
                        rows = xt[:, TT * h + 2 * b:TT * h + 2 * b + 2, :].rearrange("p t d -> p (t d)")
                        dve.tensor_tensor(rows, acc[2 * h + b][:, :], rows, ALU.add).then_inc(resid, 1)
                    dve.wait_ge(resid, 2 * (h + 1))
                for t in range(TT):
                    dve.bn_stats(stat[:, t, :], xt[:, TT * h + t, :]).then_inc(stats, 1)
                for t in range(TT):
                    dve.wait_ge(stats, TT * n + t + 1)
                    dve.bn_aggr(mv[:, t, :], stat[:, t, :]).then_inc(moments, 1)
                dve.wait_ge(moments, TT * (n + 1))
                dve.tensor_scalar(var_eps[:, :], mv[:, :, 1], EPS, None, ALU.add).then_inc(vars_ready, 1)

            def norm_apply(n):
                h = n % 2
                dve.wait_ge(rstds, n + 1)
                if n >= 1:
                    dve.wait_ge(turned, KD * n)
                for t in range(TT):
                    dve.tensor_scalar(hn[:, t, :], xt[:, TT * h + t, :], mv[:, t, 0:1], rstd[:, t:t + 1],
                                      ALU.subtract, ALU.mult).then_inc(normed, 1)

            def turn_lo(n, k, src):
                s, h = n // 2, n % 2
                dve.wait_ge(ht_his, KD * n + k + 1)
                dve.tensor_tensor(ht_lo[s][:, k, TH * h:TH * h + TH], src[:, :],
                                  f32(ht_hi[s][:, k, TH * h:TH * h + TH]), ALU.subtract).then_inc(ht_los, 1)

            def expert_ids(h):
                cols = slice(TH * h, TH * h + TH)
                if h == 0:
                    dve.wait_ge(ids_in, 16)
                dve.tensor_scalar(ids[:, cols], ids_raw[:, cols], float(IDS_PER_EXPERT), None,
                                  ALU.is_ge).then_inc(ids_step, 1)
                for e in range(2, EA):
                    dve.wait_ge(ids_step, (EA - 1) * h + e - 1)
                    dve.scalar_tensor_tensor(out=ids[:, cols], in0=ids_raw[:, cols],
                                             scalar=float(e * IDS_PER_EXPERT), in1=ids[:, cols],
                                             op0=ALU.is_ge, op1=ALU.add).then_inc(ids_step, 1)

            LINKS = 15

            def link(h, i, ins):
                ins.then_inc(route, 1)
                dve.wait_ge(route, LINKS * h + i + 1)

            def bc(ap):
                return ap.unsqueeze(2).broadcast_to([P, TT, EB])

            def route_logits(h):
                dve.wait_ge(gated, h + 1)
                if h >= 1:
                    dve.wait_ge(exps, h)
                link(h, 0, dve.tensor_reduce(
                    logit[:, :, :], work[3][:, 0:TT * 2 * EB].rearrange("p (t s e) -> p t e s", t=TT, s=2),
                    AX_X, ALU.add))
                link(h, 1, dve.tensor_reduce(lmax[:, :], logit[:, :, :], AX_X, ALU.max))
                dve.tensor_tensor(lsub[:, :, :], logit[:, :, :], bc(lmax[:, :]),
                                  ALU.subtract).then_inc(shifted, 1)

            def route_weights(h):
                dve.wait_ge(exps, h + 1)
                link(h, 2, dve.tensor_reduce(lsum[:, :], lexp[:, :, :], AX_X, ALU.add))
                link(h, 3, dve.reciprocal(lrec[:, :], lsum[:, :]))
                link(h, 4, dve.tensor_tensor(score[:, :, :], lexp[:, :, :], bc(lrec[:, :]), ALU.mult))
                for t in range(TT):
                    ins = dve.max(top_w[:, t, :], score[:, t, :])
                link(h, 5, ins)
                for t in range(TT):
                    ins = dve.max_index(top_i[:, t, :], top_w[:, t, :], score[:, t, :])
                link(h, 6, ins)
                link(h, 7, dve.tensor_copy(top_if[:, :, :], top_i[:, :, 0:TOP]))
                for r in range(TOP):
                    ins = dve.tensor_tensor(hit[:, r, :, :], iota, bc(top_if[:, :, r]), ALU.is_equal)
                link(h, 8, ins)
                for r in range(TOP):
                    ins = dve.tensor_tensor(part[:, r, :, :], hit[:, r, :, :], bc(top_w[:, :, r]), ALU.mult)
                link(h, 9, ins)
                link(h, 10, dve.tensor_tensor(dense[:, :, :], part[:, 0, :, :], part[:, 1, :, :], ALU.add))
                link(h, 11, dve.tensor_copy(dense_r[:, :, :], dense[:, :, :]))
                if h == 0:
                    dve.wait_ge(fills, 3)
                else:
                    dve.wait_ge(dense_turned, h)
                dve.tensor_copy(dense_hl[:, :, 0:EB], f32(dense_r[:, :, :])).then_inc(dense_ready, 1)
                dve.tensor_tensor(dense_hl[:, :, EB:2 * EB], dense[:, :, :], f32(dense_r[:, :, :]),
                                  ALU.subtract).then_inc(dense_ready, 1)
                dve.wait_ge(dense_ready, 2 * (h + 1))
                dve.sem_inc(route, LINKS - 12)

            def hidden_lo(n):
                dve.wait_ge(hid_his, n + 1)
                if n >= 3:
                    dve.wait_ge(downs, n - 2)
                dve.tensor_tensor(h_lo[n % 3][:, :], hb[:, n % 2, :], f32(h_hi[n % 3][:, :]),
                                  ALU.subtract).then_inc(hid_los, 1)

            def output(h):
                dve.wait_ge(downs, B0 + TILES_B * (h + 1))
                for b in range(2):
                    rows = xt[:, TT * h + 2 * b:TT * h + 2 * b + 2, :].rearrange("p t d -> p (t d)")
                    dve.tensor_tensor(rows, acc[2 * h + b][:, :], rows, ALU.add).then_inc(summed, 1)

            norm_stats(0)
            expert_ids(0)
            norm_apply(0)
            for k in range(KD):
                turn_lo(0, k, work[2 + k])
            for n in range(STEPS):
                h_in = hb[:, n % 2, :]
                if n < B0:
                    h, e = half_a(n), n % TILES_A // (FA // P)
                    dve.wait_ge(up_a, n + 1)
                    if n == 0:
                        dve.wait_ge(ids_step, EA - 1)
                    if n == 1:
                        dve.wait_ge(ids_step, 2 * (EA - 1))
                    if n >= 2:
                        dve.wait_ge(silus, n - 1)
                        dve.wait_ge(hiddens, n - 1)
                    dve.scalar_tensor_tensor(out=tm[:, n % 2, :], in0=ids[:, TH * h:TH * h + TH],
                                             scalar=float(e), in1=work[n % 2][:, :], op0=ALU.is_equal,
                                             op1=ALU.mult).then_inc(masked, 1)
                    if n >= 1:
                        hidden_lo(n - 1)
                    dve.wait_ge(silus, n + 1)
                    if n >= 2:
                        dve.wait_ge(hid_los, n - 1)
                    dve.tensor_tensor(h_in, sg[:, n % 2, :], tm[:, n % 2, :], ALU.mult).then_inc(hiddens, 1)
                else:
                    hidden_lo(n - 1)
                    gate = sg[:, n % 2, :]
                    dve.wait_ge(silus, n + 1)
                    if routed(n):
                        dve.wait_ge(spread, routed_before(n) + 1)
                        dve.tensor_tensor(tm[:, n % 2, :], work[2][:, :], gate, ALU.mult).then_inc(weighted, 1)
                        dve.wait_ge(weighted, routed_before(n) + 1)
                        gate = tm[:, n % 2, :]
                    dve.wait_ge(up_b, n - B0 + 1)
                    dve.wait_ge(hid_los, n - 1)
                    dve.tensor_tensor(h_in, work[1][:, :], gate, ALU.mult).then_inc(hiddens, 1)
                if n == AT_LN1_STATS:
                    norm_stats(1)
                    expert_ids(1)
                if n == AT_LN1_NORM:
                    norm_apply(1)
                    dve.wait_ge(g_in, 16)
                    dve.tensor_copy(g_hl[:, :, 0:EB], g_raw[:, :, :]).then_inc(g_his, 1)
                    dve.wait_ge(g_his, 1)
                    dve.tensor_tensor(g_hl[:, :, EB:2 * EB], g_raw[:, :, :], f32(g_hl[:, :, 0:EB]),
                                      ALU.subtract).then_inc(g_los, 1)
                if n == AT_LN1_TURN:
                    for k in range(KD):
                        turn_lo(1, k, work[2 + k])
                if n == AT_LN2A_STATS:
                    norm_stats(2)
                if n == AT_LN2A_NORM:
                    norm_apply(2)
                if n == AT_LN2A_TURN:
                    for k in range(KD):
                        turn_lo(2, k, work[2 + k])
                if n == AT_GATE_A:
                    dve.wait_ge(cst_in, 16)
                    route_logits(0)
                if n == AT_ROUTE_A:
                    route_weights(0)
                if n == AT_LN2B_STATS:
                    norm_stats(3)
                if n == AT_LN2B_NORM:
                    norm_apply(3)
                for k in range(KD):
                    if n == AT_LN2B_TURN + k:
                        turn_lo(3, k, work[3])
                if n == AT_GATE_B:
                    route_logits(1)
                if n == AT_ROUTE_B:
                    route_weights(1)
                if n == AT_OUT_A:
                    output(0)
            hidden_lo(STEPS - 1)
            output(1)

        @block.tensor
        def _(pe):
            def turn(n, k, dst):
                pe.wait_ge(normed, TT * (n + 1))
                if n >= 1:
                    pe.wait_ge(ht_los, KD * n - KD + k + 1)
                for t in range(TT):
                    mm = pe.transpose(dst[:, P * t:P * t + P], hn[:, t, P * k:P * k + P], ident)
                mm.then_inc(turned, 1)

            def up_passes(dst, hi, lo, s, h):
                cols = slice(TH * h, TH * h + TH)
                for k in range(KD):
                    for w, v in ((hi, ht_hi[s]), (hi, ht_lo[s]), (lo, ht_hi[s])):
                        mm = pe.matmul(dst[:, :], w(k), v[:, k, cols], start=(k == 0 and w is hi and v is ht_hi[s]),
                                       stop=(k == KD - 1 and w is lo))
                return mm

            def up(n):
                if n < B0:
                    h, e, f = half_a(n), n % TILES_A // (FA // P), n % (FA // P)
                    pe.wait_ge(c_los, e + 1)
                    pe.wait_ge(ht_los, KD * (h + 1))
                    if n >= 2:
                        pe.wait_ge(masked, n - 1)
                    up_passes(work[n % 2], lambda k: c_hi[:, e, D * k + P * f:D * k + P * f + P],
                              lambda k: c_lo[:, e, D * k + P * f:D * k + P * f + P], 0, h).then_inc(up_a, 1)
                    return
                h, g = half_b(n), tile_b(n)
                if routed(n):
                    r = routed_before(n)
                    if r == 0:
                        pe.wait_ge(sel_ready, 1)
                    pe.wait_ge(dense_copied, h + 1)
                    if r >= 1:
                        pe.wait_ge(weighted, r)
                    j = g - SHARED_TILES
                    pe.matmul(work[2][:, :], sel_r[:, P * j:P * j + P], dense_t[h][:, :],
                              start=True, stop=True).then_inc(spread, 1)
                pe.wait_ge(w_los, g + 1)
                pe.wait_ge(ht_los, KD * (2 + h + 1))
                if n == B0:
                    pe.wait_ge(masked, STEPS_A)
                else:
                    pe.wait_ge(silus, n)
                up_passes(work[0], lambda k: w_hi[:, g, P * k:P * k + P],
                          lambda k: w_lo[:, g, P * k:P * k + P], 1, h).then_inc(up_a, 1)
                if n > B0:
                    pe.wait_ge(hiddens, n)
                up_passes(work[1], lambda k: w_hi[:, g, P * (KD + k):P * (KD + k) + P],
                          lambda k: w_lo[:, g, P * (KD + k):P * (KD + k) + P], 1, h).then_inc(up_b, 1)

            def down(n):
                if n < B0:
                    h, first, last = half_a(n), n % TILES_A == 0, n % TILES_A == TILES_A - 1
                    e, f = n % TILES_A // (FA // P), n % (FA // P)
                    hi, lo = c_hi[:, e, D * f:D * f + D], c_lo[:, e, D * f:D * f + D]
                else:
                    h, g = half_b(n), tile_b(n)
                    first, last = g == 0, g == TILES_B - 1
                    hi, lo = w_hi[:, g, WCOLS - D:WCOLS], w_lo[:, g, WCOLS - D:WCOLS]
                    if first:
                        pe.wait_ge(resid, 2 * (h + 1))
                pe.wait_ge(hid_los, n + 1)
                for t in range(TT):
                    rows, cols = slice(P * t, P * t + P), slice(D * (t % 2), D * (t % 2) + D)
                    for i, (v, w) in enumerate(((h_hi, hi), (h_hi, lo), (h_lo, hi))):
                        mm = pe.matmul(acc[2 * h + t // 2][:, cols], v[n % 3][:, rows], w,
                                       start=(first and i == 0 and t % 2 == 0), stop=(last and i == 2),
                                       skip_group_check=True)
                mm.then_inc(downs, 1)

            def gate(h):
                pe.wait_ge(g_los, 1)
                pe.wait_ge(ht_los, KD * (2 + h + 1))
                for t in range(TT):
                    rows = slice(TH * h + P * t, TH * h + P * t + P)
                    for k in range(KD):
                        for v in (ht_hi[1], ht_lo[1]):
                            mm = pe.matmul(work[3][:, 2 * EB * t:2 * EB * t + 2 * EB], v[:, k, rows], g_hl[:, k, :],
                                           start=(k == 0 and v is ht_hi[1]), stop=(k == KD - 1 and v is ht_lo[1]))
                mm.then_inc(gated, 1)

            def dense_turn(h):
                pe.wait_ge(dense_ready, 2 * (h + 1))
                for t in range(TT):
                    mm = pe.transpose(work[3][:, P * t:P * t + P], dense_hl[:, t, :], ident)
                mm.then_inc(dense_turned, 1)

            pe.wait_ge(cst_in, 16)
            for k in range(KD):
                turn(0, k, work[2 + k])
            for n in range(STEPS):
                up(n)
                if n == AT_LN1_TURN:
                    for k in range(KD):
                        turn(1, k, work[2 + k])
                if n == AT_LN2A_TURN:
                    for k in range(KD):
                        turn(2, k, work[2 + k])
                if n == AT_GATE_A:
                    gate(0)
                if n == AT_DENSE_A:
                    dense_turn(0)
                for k in range(KD):
                    if n == AT_LN2B_TURN + k:
                        if k == 0:
                            pe.wait_ge(dense_copied, 1)
                        else:
                            pe.wait_ge(ht_los, KD * 3 + k)
                        turn(3, k, work[3])
                if n == AT_GATE_B:
                    gate(1)
                if n == AT_DENSE_B:
                    dense_turn(1)
                if n < B0:
                    if n >= LAG_A:
                        down(n - LAG_A)
                else:
                    if n == B0:
                        down(n - LAG_A)
                    down(n - 1)
            down(STEPS - 1)


def kernel(**inputs):
    import numpy as np
    import concourse.bacc as bacc
    from concourse.bass_utils import run_bass_kernel_spmd as run

    x = np.asarray(inputs["x"])
    tok = np.ascontiguousarray(np.asarray(inputs["itok_BxS_13_99985"]).reshape(T))
    c = np.asarray(inputs["ctx_2048"])
    ctx_t = np.ascontiguousarray(c.transpose(0, 2, 1).reshape(EA, KD, P, D).transpose(0, 2, 1, 3).reshape(EA, P, KD * D))

    def hidden_rows(shared, experts):
        s = np.zeros((SHARED_TILES * P, D), shared.dtype)
        s[:SHARED] = shared
        return np.concatenate([s, experts.reshape(EB * IB, D)]).reshape(TILES_B, P, D)

    def width_major(rows):
        return rows.transpose(0, 2, 1).reshape(TILES_B, KD, P, P).transpose(0, 2, 1, 3).reshape(TILES_B, P, KD * P)

    a = {k: np.asarray(inputs["L0_ffn_" + k]) for k in ("gate_w", "w1", "w2", "w3", "sw1", "sw2", "sw3")}
    w_b = np.ascontiguousarray(np.concatenate([
        width_major(hidden_rows(a["sw1"], a["w1"])), width_major(hidden_rows(a["sw3"], a["w3"])),
        hidden_rows(a["sw2"].T, a["w2"].transpose(0, 2, 1))], axis=2))
    gate_t = np.ascontiguousarray(a["gate_w"].T.reshape(KD, P, EB).transpose(1, 0, 2))
    consts = np.concatenate([np.eye(P, dtype=np.float32),
                             np.tile(np.arange(EB, dtype=np.float32), (P, TT))], axis=1)
    owner = np.arange(EB * IB) // IB
    sel = np.zeros((P, EB * IB), np.float32)
    sel[:2 * EB] = np.tile(owner == np.arange(EB)[:, None], (2, 1))

    nc = bacc.Bacc("TRN2", target_bir_lowering=False, num_devices=1)
    arrays, args = {}, []
    for name, v in (("x", np.ascontiguousarray(x.reshape(T, D))), ("tok", tok), ("ctx_t", ctx_t),
                    ("gate_t", gate_t), ("w_b", w_b), ("consts", consts), ("sel", sel)):
        arrays[name] = v
        args.append(nc.dram_tensor(name, v.shape, mybir.dt.from_np(v.dtype), kind="ExternalInput").ap())
    args.append(nc.dram_tensor("out", (T, D), F32, kind="ExternalOutput").ap())
    build(nc, *args)
    r = run(nc, [arrays], core_ids=[0])
    return r.results[0]["out"].reshape(x.shape)
```

```python
from contextlib import ExitStack

import concourse.bass as bass
from concourse import mybir

P = 128
T, D = 1024, 256
KD = D // P
HALVES = 2
TH = T // HALVES
TT = TH // P
EA = 4
FA = 256
IDS_PER_EXPERT = 12500 // EA
EB, IB = 8, 176
SHARED = 2 * IB
SHARED_TILES = -(-SHARED // P)
SHARED_COLS = 2 * KD * P + D
FB = -(-IB // P)
UPC = 2 * IB
EXPERT_COLS = KD * UPC + FB * D
BLOCKS = SHARED_TILES + EB
EPS = 1e-5
E_FLOAT = 2.718281828459045
TOP = 2
TILES_0 = TH * TOP // P + EB - 1
TILES = T * TOP // P + EB - 1
ROW = D + 1
EMPTIED = 3
SLOT_INS, SLOT_OUTS = 5, 4
NO_ROW = 1 << 20

TILES_A = EA * FA // P
STEPS_A = HALVES * TILES_A
STEPS_B = HALVES * SHARED_TILES
STEPS = STEPS_A + STEPS_B
LAG_A = 2
RAW = 2

READ_0, COMBINE_0 = TILES_0 + SLOT_INS, TILES_0 + SLOT_INS
B0 = STEPS_A
LN1B = dict(stats=0, apply=3, turn=5, copy=6)
LN2A = dict(stats=9, apply=11, turn=12, copy=13)
PICK_A, COUNT_A, SLOTS_A = 14, 15, 15
VECTOR_LO = (1, 3, 5, 7, 8, 10, 11, 12, 13, 14, 15) + tuple(range(STEPS_A, STEPS))
LO_AT = [1, 3, 5, 6, 8, 10, 12, 14]
POOL_BLOCKS_A = len(LO_AT)
POOL_BLOCKS = 10
HI_AT = [1, 2, 4, 5, 7, 9, 11, 13, 15, 18, 19]
WARM_UPS = 18
RSQRT_3 = (0, 1, 0)
WEIGHTS_AT = (8, 10)

F32 = mybir.dt.float32
F32R = mybir.dt.float32r
I32 = mybir.dt.int32
U32 = mybir.dt.uint32
BF16 = mybir.dt.bfloat16
ALU = mybir.AluOpType
ACT = mybir.ActivationFunctionType
AX_X = mybir.AxisListType.X


def build(nc, x, tok, ctx_t, gate_t, w_shared, w_expert, consts, slot_rows, result_rows, out):
    x_tiles = x.rearrange("(t p) d -> p t d", p=P)
    out_tiles = out.rearrange("(t p) d -> p t d", p=P)

    with ExitStack() as ctx:
        def sb(name, shape, dt=F32):
            return ctx.enter_context(nc.sbuf_tensor(name, shape, dt))

        def bank(name):
            return ctx.enter_context(nc.psum_tensor(name, [P, 512], F32))

        def sem(name):
            return ctx.enter_context(nc.semaphore(name))

        xt = sb("xt", [P, HALVES * TT, D])
        ids = sb("ids", [P, T])
        cst = sb("cst", [P, 2 * P + TT * EB + 2 * EB * EB + TILES + TOP * HALVES * TT])
        at = 0
        views = []
        for cols in (P, P, TT * EB, EB * EB, EB * EB, TILES, TOP * HALVES * TT):
            views.append(cst[:, at:at + cols])
            at += cols
        ident, before_f, iota, starts, lower, tile_no, row_no = views
        iota = iota.rearrange("p (t e) -> p t e", t=TT)
        starts = starts.rearrange("p (e k) -> p e k", e=EB)
        lower = lower.rearrange("p (e f) -> p e f", e=EB)
        row_no = row_no.rearrange("p (r t) -> p r t", r=TOP)
        before_b = sb("before_b", [P, P], BF16)
        ones_b = sb("ones_b", [P, P], BF16)
        scratch = sb("scratch", [P, TT * TOP * ROW])
        c_raw = scratch[:, 0:EA * KD * D].rearrange("p (e n) -> p e n", e=EA)
        c_hi = sb("c_hi", [P, EA, KD * D], F32R)
        c_lo = sb("c_lo", [P, EA, KD * D], F32R)
        rows = scratch[:, :].rearrange("p (r t n) -> p r t n", r=TOP, t=TT)
        empty = sb("empty", [P, ROW])
        w_raw = sb("w_raw", [P, RAW, EXPERT_COLS])
        ws_hi = sb("ws_hi", [P, SHARED_TILES, SHARED_COLS], F32R)
        ws_lo = sb("ws_lo", [P, SHARED_TILES, SHARED_COLS], F32R)
        we_hi = sb("we_hi", [P, EB, EXPERT_COLS], F32R)
        we_lo = sb("we_lo", [P, EB, EXPERT_COLS], F32R)
        g_raw = sb("g_raw", [P, KD, EB])
        g_hl = sb("g_hl", [P, KD, 2 * EB], F32R)
        stat = sb("stat", [P, TT, 6])
        mv = sb("mv", [P, TT, 2])
        var_eps = sb("var_eps", [P, TT])
        rstd = sb("rstd", [P, TT])
        power = sb("power", [P, TT])
        base_e = sb("base_e", [P, TT, EB])
        hn = sb("hn", [P, TT, D])
        ht_hi = [sb(f"ht_hi{s}", [P, KD, T], F32R) for s in range(2)]
        ht_lo = [sb(f"ht_lo{s}", [P, KD, T], F32R) for s in range(2)]
        tm = sb("tm", [P, 2, TH])
        sg = sb("sg", [P, 2, TH])
        hb = sb("hb", [P, 2, TH])
        ids_raw = w_raw[:, 1, 0:T].bitcast(I32)
        h_hi = [sb(f"h_hi{s}", [P, TH], F32R) for s in range(3)]
        h_lo = [sb(f"h_lo{s}", [P, TH], F32R) for s in range(3)]
        logit = sb("logit", [P, TT, EB])
        lmax = sb("lmax", [P, TT])
        lsub = sb("lsub", [P, HALVES, TT, EB])
        lexp = sb("lexp", [P, HALVES, TT, EB])
        lsum = sb("lsum", [P, TT])
        lrec = sb("lrec", [P, TT])
        top_w = sb("top_w", [P, TT, 8])
        top_i = sb("top_i", [P, TT, 8], U32)
        top_if = sb("top_if", [P, TT, TOP])
        hit = sb("hit", [P, HALVES, TOP, TT * EB])
        chosen = sb("chosen", [P, HALVES * TT, EB], BF16)
        product = sb("product", [P, TOP, TT * EB])
        picked_e = sb("picked_e", [P, TOP, TT])
        weight = sb("weight", [P, HALVES, TOP, TT])
        over = sb("over", [P, EB, EB])
        n_tiles = sb("n_tiles", [P, HALVES, EB])
        first = sb("first", [P, HALVES, EB])
        below = sb("below", [P, EB, EB])
        room = sb("room", [P, EB])
        beyond = sb("beyond", [P, EB])
        jump = sb("jump", [P, EB])
        all_0 = sb("all_0", [P, 1])
        place = sb("place", [P, TT, EB])
        moved = sb("moved", [P, TT, EB])
        slot_f = sb("slot_f", [P, TOP, TT])
        slot = sb("slot", [P, HALVES, TOP, TT], U32)
        passed = ids[0:1, 0:TILES * HALVES * EB].rearrange("p (i f) -> p i f", i=TILES)
        passed_n = sb("passed_n", [1, TILES])
        expert_f = sb("expert_f", [1, TILES])
        expert = sb("expert", [1, TILES], I32)
        slot_in = [tm[:, :, :].rearrange("p a n -> p (a n)")[:, ROW * a:ROW * a + ROW] for a in range(3)]
        slot_in += [sg[:, a, IB:IB + ROW] for a in range(2)]
        act_s = sg[:, :, 0:IB]
        hid_s = hb[:, :, 0:FB * P]
        result_row = sb("result_row", [P, TILES], U32)
        slot_out = hn
        slot_hi, slot_lo, hidt_hi, hidt_lo = (
            [v[:, k, D * a:D * a + D] for a in range(2)] for v in (ht_hi[0], ht_lo[0]) for k in range(KD))
        res = [scratch[:, 0:HALVES * TT * D].rearrange("p (t d) -> p t d", d=D),
               w_raw[:, :, :].rearrange("p a n -> p (a n)")[:, 0:HALVES * TT * D].rearrange("p (t d) -> p t d", d=D)]

        work = [bank(f"work{b}") for b in range(4)]
        acc = [bank(f"acc{b}") for b in range(4)]

        x_in = [sem(f"x_in{i}") for i in range(2 * HALVES)]
        ids_in, cst_in, g_in = sem("ids_in"), sem("cst_in"), sem("g_in")
        c_in = [sem(f"c_in{e}") for e in range(EA)]
        w_in = [sem(f"w_in{s}") for s in range(RAW)]
        empty_ready = sem("empty_ready")
        emptied = sem("emptied")
        rows_out = sem("rows_out")
        slot_ins = [sem(f"slot_ins{a}") for a in range(SLOT_INS)]
        results_out = [sem(f"results_out{a}") for a in range(SLOT_OUTS)]
        res_in = [sem(f"res_in{i}") for i in range(2 * HALVES)]
        out_done = sem("out_done")
        fills = sem("fills")
        resid = sem("resid")
        doubled = sem("doubled")
        stats, moments, vars_ready = sem("stats"), sem("moments"), sem("vars_ready")
        rstds, normed = sem("rstds"), sem("normed")
        turned = sem("turned")
        ht_his, ht_los = sem("ht_his"), sem("ht_los")
        ids_step, ids_ready = sem("ids_step"), sem("ids_ready")
        c_his, c_los, w_his = sem("c_his"), sem("c_los"), sem("w_his")
        w_los_pool, w_los_dve = sem("w_los_pool"), sem("w_los_dve")
        g_his, g_los, before_ready = sem("g_his"), sem("g_los"), sem("before_ready")
        up_a = sem("up_a")
        up_b = sem("up_b")
        masked = sem("masked")
        silus, hiddens = sem("silus"), sem("hiddens")
        hid_his = sem("hid_his")
        hid_los_v, hid_los_p = sem("hid_los_v"), sem("hid_los_p")
        downs = sem("downs")
        gated, counted = sem("gated"), sem("counted")
        link_done = sem("link_done")
        shifted, exps = sem("shifted"), sem("exps")
        chosens, slots_ready, marked = sem("chosens"), sem("slots_ready"), sem("marked")
        experts_ready = sem("experts_ready")
        weight_link, weights_ready = sem("weight_link"), sem("weights_ready")
        shared_added = sem("shared_added")
        marks_read = sem("marks_read")
        slot_turned, slot_his, slot_los = sem("slot_turned"), sem("slot_his"), sem("slot_los")
        slot_up, slot_silu, slot_hid = sem("slot_up"), sem("slot_silu"), sem("slot_hid")
        hid_zero = sem("hid_zero")
        hid_turned, hidt_his, hidt_los = sem("hid_turned"), sem("hidt_his"), sem("hidt_los")
        slot_down, slot_done = sem("slot_down"), sem("slot_done")
        combined = sem("combined")
        results = sem("results")

        block = ctx.enter_context(nc.Block())

        def half_a(n):
            return n // TILES_A

        def half_b(n):
            return (n - B0) // SHARED_TILES

        def tile_b(n):
            return (n - B0) % SHARED_TILES

        def block_cols(b):
            return SHARED_COLS if b < SHARED_TILES else EXPERT_COLS

        def block_hi(b):
            return ws_hi[:, b, :] if b < SHARED_TILES else we_hi[:, b - SHARED_TILES, :]

        def block_lo(b):
            return ws_lo[:, b, :] if b < SHARED_TILES else we_lo[:, b - SHARED_TILES, :]

        def block_split(eng, b):
            if b < POOL_BLOCKS:
                eng.wait_ge(w_los_pool, b + 1)
            else:
                eng.wait_ge(w_los_dve, b - POOL_BLOCKS + 1)

        def pair(i):
            return xt[:, 2 * i:2 * i + 2, :].rearrange("p t d -> p (t d)")

        def hidden_split(eng, n):
            if n in VECTOR_LO:
                eng.wait_ge(hid_los_v, VECTOR_LO.index(n) + 1)
            else:
                eng.wait_ge(hid_los_p, n + 1 - sum(v < n for v in VECTOR_LO))

        def f32(ap):
            return ap.bitcast(F32)

        @block.sync
        def _(sp):
            sp.dma_start(xt[:, 0:2, :], x_tiles[:, 0:2, :]).then_inc(x_in[0], 16)
            sp.dma_start(ids_raw, tok.partition_broadcast(P)).then_inc(ids_in, 16)
            sp.dma_start(c_raw[:, 0, :], ctx_t[0]).then_inc(c_in[0], 16)
            for i in range(2, 4):
                sp.dma_start(xt[:, 2 * i:2 * i + 2, :], x_tiles[:, 2 * i:2 * i + 2, :]).then_inc(x_in[i], 16)
            for e in range(1, EA):
                sp.dma_start(c_raw[:, e, :], ctx_t[e]).then_inc(c_in[e], 16)
            for b in range(BLOCKS):
                if b == 1:
                    sp.wait_ge(ids_step, HALVES * (EA - 1))
                if b >= RAW:
                    block_split(sp, b - RAW)
                src = w_shared[b] if b < SHARED_TILES else w_expert[b - SHARED_TILES]
                sp.dma_start(w_raw[:, b % RAW, 0:block_cols(b)], src).then_inc(w_in[b % RAW], 16)
                if b == 0:
                    sp.wait_ge(empty_ready, 2)
                i, j = EMPTIED * b, min(EMPTIED * b + EMPTIED, TILES)
                if i < j:
                    sp.dma_start(slot_rows[P * i:P * j, :].rearrange("(i p) n -> p i n", p=P),
                                 empty[:, :].unsqueeze(1).broadcast_to([P, j - i, ROW])).then_inc(emptied, 16)
            sp.wait_ge(rows_out, 16 * HALVES * TOP * TT)

            def read_slots(i):
                if i == 3:
                    sp.wait_ge(hiddens, STEPS)
                if i >= SLOT_INS:
                    sp.wait_ge(slot_turned, i - SLOT_INS + 1)
                    sp.wait_ge(marks_read, i - SLOT_INS + 1)
                sp.dma_start(slot_in[i % SLOT_INS], slot_rows[P * i:P * i + P, :]).then_inc(
                    slot_ins[i % SLOT_INS], 16)

            def read_results(h, b, c):
                last = (TILES_0 if h == 0 else TILES) - 1
                for a in range(SLOT_OUTS):
                    i = last - (last - a) % SLOT_OUTS
                    sp.wait_ge(results_out[a], 16 * (i // SLOT_OUTS + 1))
                t = TT * h + 2 * b
                sp.dma_start(res[c][:, t:t + 2, :], result_rows[T * c + P * t:T * c + P * (t + 2), :].rearrange(
                    "(t p) d -> p t d", p=P)).then_inc(res_in[2 * h + b], 16)

            def write(h):
                for b in range(2):
                    sp.wait_ge(combined, TOP * (2 * h + b + 1))
                    t = TT * h + 2 * b
                    sp.dma_start(out_tiles[:, t:t + 2, :], xt[:, t:t + 2, :]).then_inc(out_done, 16)

            for i in range(TILES):
                read_slots(i)
                if READ_0 <= i < READ_0 + 2:
                    for c in range(TOP):
                        read_results(0, i - READ_0, c)
            write(0)
            for b in range(2):
                for c in range(TOP):
                    read_results(1, b, c)
            write(1)
            sp.wait_ge(out_done, 16 * 2 * HALVES)

        @block.gpsimd
        def _(pool):
            pool.memset(ones_b[:, :], 1.0).then_inc(fills, 1)
            pool.memset(power[:, :], -0.5).then_inc(fills, 1)
            pool.memset(base_e[:, :, :], E_FLOAT).then_inc(fills, 1)
            pool.memset(empty[:, 0:D], 0.0).then_inc(empty_ready, 1)
            pool.memset(empty[:, D:ROW].bitcast(U32), NO_ROW).then_inc(empty_ready, 1)
            pool.wait_ge(fills, 3)

            def rsqrt(n):
                pool.wait_ge(vars_ready, n + 1)
                if n >= 1:
                    pool.wait_ge(normed, TT * n)
                pool.tensor_tensor(rstd[:, :], var_eps[:, :], power[:, :], ALU.pow).then_inc(rstds, 1)

            def exponent(h, t):
                pool.wait_ge(shifted, h + 1)
                pool.tensor_tensor(lexp[:, h, t, :], base_e[:, t, :], lsub[:, h, t, :], ALU.pow).then_inc(exps, 1)

            def weights_lo(b):
                pool.wait_ge(w_his, b + 1)
                cols = block_cols(b)
                pool.tensor_tensor(block_lo(b), w_raw[:, b % RAW, 0:cols], f32(block_hi(b)),
                                   ALU.subtract).then_inc(w_los_pool, 1)

            def scatter_rows(h):
                if h == 0:
                    pool.wait_ge(emptied, 16 * -(-TILES // EMPTIED))
                pool.wait_ge(slots_ready, h + 1)
                pool.wait_ge(marked, h + 1)
                for c in range(TOP):
                    if h == 0 and c == 0:
                        pool.wait_ge(normed, TT * 3)
                    else:
                        pool.wait_ge(doubled, 1 if h == 0 else c + 2)
                    for t in range(TT):
                        pool.indirect_dma_start(slot_rows, bass.IndirectOffsetOnAxis(slot[:, h, c, t:t + 1], 0),
                                                rows[:, c, t, :], None).then_inc(rows_out, 16)
                        if (h, c, t) == RSQRT_3:
                            rsqrt(3)

            def scatter_results(i):
                pool.wait_ge(slot_done, i + 1)
                pool.indirect_dma_start(result_rows, bass.IndirectOffsetOnAxis(result_row[:, i:i + 1], 0),
                                        slot_out[:, i % SLOT_OUTS, :], None, bounds_check=TOP * T - 1,
                                        oob_is_err=False).then_inc(results_out[i % SLOT_OUTS], 16)

            rsqrt(0)
            for e in range(EA):
                pool.wait_ge(c_his, e + 1)
                pool.tensor_tensor(c_lo[:, e, :], c_raw[:, e, :], f32(c_hi[:, e, :]),
                                   ALU.subtract).then_inc(c_los, 1)
            for n in range(STEPS_A):
                if n not in VECTOR_LO:
                    pool.wait_ge(hid_his, n + 1)
                    if n >= 3:
                        pool.wait_ge(downs, n - 2)
                    pool.tensor_tensor(h_lo[n % 3][:, :], hb[:, n % 2, :], f32(h_hi[n % 3][:, :]),
                                       ALU.subtract).then_inc(hid_los_p, 1)
                if n == LN1B["stats"]:
                    rsqrt(1)
                if n == LN2A["stats"]:
                    rsqrt(2)
                if n in LO_AT:
                    weights_lo(LO_AT.index(n))
            scatter_rows(0)
            for b in range(POOL_BLOCKS_A, POOL_BLOCKS):
                weights_lo(b)
            scatter_rows(1)
            for i in range(TILES):
                if i < HALVES * TT:
                    exponent(i // TT, i % TT)
                scatter_results(i)

        @block.scalar
        def _(act):
            act.dma_start(xt[:, 2:4, :], x_tiles[:, 2:4, :]).then_inc(x_in[1], 16)
            act.dma_start(cst[:, :], consts).then_inc(cst_in, 16)
            act.dma_start(g_raw[:, :, :], gate_t).then_inc(g_in, 16)
            nc.scalar.preload_act_table(ACT.Silu)

            def ctx_hi(e):
                act.wait_ge(c_in[e], 16)
                act.activation(c_hi[:, e, :], c_raw[:, e, :], ACT.Copy).then_inc(c_his, 1)

            def turn_hi(n, k, src):
                s, h = n // 2, n % 2
                act.wait_ge(turned, KD * n + k + 1)
                act.activation(ht_hi[s][:, k, TH * h:TH * h + TH], src[:, :], ACT.Copy).then_inc(ht_his, 1)

            def double(h):
                act.wait_ge(normed, TT * (3 + h))
                if h == 0:
                    act.activation(rows[:, 1, :, 0:D], rows[:, 0, :, 0:D], ACT.Copy).then_inc(doubled, 1)
                    return
                act.wait_ge(rows_out, 16 * TOP * TT)
                for c in range(TOP):
                    act.activation(rows[:, c, :, 0:D], hn[:, :, :], ACT.Copy).then_inc(doubled, 1)

            ctx_hi(0)
            for k in range(KD):
                turn_hi(0, k, work[2 + k])
            for e in range(1, EA):
                ctx_hi(e)
            act.wait_ge(cst_in, 16)
            act.activation(before_b[:, :], before_f, ACT.Copy).then_inc(before_ready, 1)
            for n in range(STEPS):
                if n < B0:
                    act.wait_ge(masked, n + 1)
                    src = tm[:, n % 2, :]
                else:
                    act.wait_ge(up_a, n + 1)
                    src = work[0][:, :]
                if n >= 2:
                    act.wait_ge(hiddens, n - 1)
                act.activation(sg[:, n % 2, :], src, ACT.Silu).then_inc(silus, 1)
                if n == LN1B["copy"]:
                    for k in range(KD):
                        turn_hi(1, k, work[2 + k])
                if n == LN2A["copy"]:
                    for k in range(KD):
                        turn_hi(2, k, work[2 + k])
                if n == B0 + 1:
                    for k in range(KD):
                        turn_hi(3, k, work[2 + k])
                act.wait_ge(hiddens, n + 1)
                if n >= 3:
                    act.wait_ge(downs, n - 2)
                act.activation(h_hi[n % 3][:, :], hb[:, n % 2, :], ACT.Copy).then_inc(hid_his, 1)
                if n in HI_AT:
                    b = HI_AT.index(n)
                    act.wait_ge(w_in[b % RAW], 16 * (b // RAW + 1))
                    act.activation(block_hi(b), w_raw[:, b % RAW, 0:block_cols(b)], ACT.Copy).then_inc(w_his, 1)
                if n == LN2A["turn"] + 1:
                    double(0)
                if n == B0 + 2:
                    double(1)

            def split_hi(dst, src, done):
                act.activation(dst, src[:, 0:D], ACT.Copy).then_inc(done, 1)

            def slot_copy(i):
                act.wait_ge(slot_turned, i + 1)
                if i >= 2:
                    act.wait_ge(slot_up, i - 1)
                split_hi(slot_hi[i % 2], work[2 + i % 2], slot_his)

            def slot_gate(i):
                act.wait_ge(slot_up, i + 1)
                if i >= 2:
                    act.wait_ge(slot_hid, i - 1)
                act.activation(act_s[:, i % 2, :], work[i % 2][:, 0:IB], ACT.Silu).then_inc(slot_silu, 1)

            def hid_copy(i):
                act.wait_ge(hid_turned, i + 1)
                if i >= 2:
                    act.wait_ge(slot_down, i - 1)
                split_hi(hidt_hi[i % 2], acc[i % 2], hidt_his)

            def slot_store(i):
                act.wait_ge(slot_down, i + 1)
                if i >= SLOT_OUTS:
                    act.wait_ge(results_out[i % SLOT_OUTS], 16 * (i // SLOT_OUTS))
                act.activation(slot_out[:, i % SLOT_OUTS, :], acc[2 + i % 2][:, 0:D], ACT.Copy).then_inc(slot_done, 1)

            slot_copy(0)
            slot_copy(1)
            for i in range(TILES + 2):
                if i < TILES:
                    slot_gate(i)
                if 1 <= i < TILES + 1:
                    hid_copy(i - 1)
                if i + 2 < TILES:
                    slot_copy(i + 2)
                if i >= 2:
                    slot_store(i - 2)

        @block.vector
        def _(dve):
            def norm_stats(n, b):
                h = n % 2
                if n < 2:
                    dve.wait_ge(x_in[2 * h + b], 16)
                else:
                    dve.wait_ge(downs, TILES_A * (h + 1))
                    rows = xt[:, TT * h + 2 * b:TT * h + 2 * b + 2, :].rearrange("p t d -> p (t d)")
                    dve.tensor_tensor(rows, acc[2 * h + b][:, :], rows, ALU.add).then_inc(resid, 1)
                    dve.wait_ge(resid, 2 * h + b + 1)
                for t in range(2 * b, 2 * b + 2):
                    dve.bn_stats(stat[:, t, :], xt[:, TT * h + t, :]).then_inc(stats, 1)
                for t in range(2 * b, 2 * b + 2):
                    dve.wait_ge(stats, TT * n + t + 1)
                    dve.bn_aggr(mv[:, t, :], stat[:, t, :]).then_inc(moments, 1)
                if b == 1:
                    dve.wait_ge(moments, TT * (n + 1))
                    dve.tensor_scalar(var_eps[:, :], mv[:, :, 1], EPS, None, ALU.add).then_inc(vars_ready, 1)

            def norm_apply(n, b):
                h = n % 2
                dve.wait_ge(rstds, n + 1)
                if n == 1:
                    dve.wait_ge(turned, KD)
                if n == 2:
                    dve.wait_ge(c_los, EA)
                for t in range(2 * b, 2 * b + 2):
                    dst = hn[:, t, :] if n != 2 else rows[:, 0, t, 0:D]
                    dve.tensor_scalar(dst, xt[:, TT * h + t, :], mv[:, t, 0:1], rstd[:, t:t + 1],
                                      ALU.subtract, ALU.mult).then_inc(normed, 1)

            def mark_rows(h):
                if h == 0:
                    dve.wait_ge(cst_in, 16)
                else:
                    dve.wait_ge(rows_out, 16 * TOP * TT)
                dve.tensor_copy(rows[:, :, :, D:ROW].bitcast(U32),
                                row_no[:, :, TT * h:TT * h + TT].unsqueeze(3)).then_inc(marked, 1)

            def turn_lo(n, k, src):
                s, h = n // 2, n % 2
                dve.wait_ge(ht_his, KD * n + k + 1)
                dve.tensor_tensor(ht_lo[s][:, k, TH * h:TH * h + TH], src[:, :],
                                  f32(ht_hi[s][:, k, TH * h:TH * h + TH]), ALU.subtract).then_inc(ht_los, 1)

            def expert_ids(h, e):
                cols = slice(TH * h, TH * h + TH)
                if e == 1:
                    if h == 0:
                        dve.wait_ge(ids_in, 16)
                    dve.tensor_scalar(ids[:, cols], ids_raw[:, cols], float(IDS_PER_EXPERT), None,
                                      ALU.is_ge).then_inc(ids_step, 1)
                    return
                dve.wait_ge(ids_step, (EA - 1) * h + e - 1)
                dve.scalar_tensor_tensor(out=ids[:, cols], in0=ids_raw[:, cols], scalar=float(e * IDS_PER_EXPERT),
                                         in1=ids[:, cols], op0=ALU.is_ge, op1=ALU.add).then_inc(ids_step, 1)

            links = [0]

            def link(ins):
                links[0] += 1
                ins.then_inc(link_done, 1)
                dve.wait_ge(link_done, links[0])

            def over_experts(ap):
                return ap.unsqueeze(2).broadcast_to([P, TT, EB])

            def choose(h):
                dve.wait_ge(gated, h + 1)
                link(dve.tensor_reduce(
                    logit[:, :, :], work[3][:, 0:TT * 2 * EB].rearrange("p (t s e) -> p t e s", t=TT, s=2),
                    AX_X, ALU.add))
                for t in range(TT):
                    ins = dve.max(top_w[:, t, :], logit[:, t, :])
                link(ins)
                for t in range(TT):
                    ins = dve.max_index(top_i[:, t, :], top_w[:, t, :], logit[:, t, :])
                link(ins)
                link(dve.tensor_copy(top_if[:, :, :], top_i[:, :, 0:TOP]))
                for c in range(TOP):
                    ins = dve.tensor_tensor(hit[:, h, c, :].rearrange("p (t e) -> p t e", t=TT), iota,
                                            over_experts(top_if[:, :, c]), ALU.is_equal)
                link(ins)
                dve.tensor_tensor(chosen[:, TT * h:TT * h + TT, :].rearrange("p t e -> p (t e)"),
                                  hit[:, h, 0, :], hit[:, h, 1, :], ALU.add).then_inc(chosens, 1)
                dve.tensor_tensor(lsub[:, h, :, :], logit[:, :, :], over_experts(top_w[:, :, 0]),
                                  ALU.subtract).then_inc(shifted, 1)

            def find_slots(h):
                dve.wait_ge(counted, h + 1)
                rank = work[2][:, 0:TT * EB].rearrange("p (t e) -> p t e", t=TT)
                count = work[2][:, TT * EB:TT * EB + EB]
                if h == 1:
                    link(dve.tensor_tensor(beyond[:, :], count, room[:, :], ALU.subtract))
                    count = beyond[:, :]
                link(dve.tensor_tensor(over[:, :, :], count.unsqueeze(2).broadcast_to([P, EB, EB]), starts,
                                       ALU.is_gt))
                link(dve.tensor_reduce(n_tiles[:, h, :], over[:, :, :], AX_X, ALU.add))
                link(dve.tensor_tensor(below[:, :, :], lower,
                                       n_tiles[:, h, :].unsqueeze(1).broadcast_to([P, EB, EB]), ALU.mult))
                link(dve.tensor_reduce(first[:, h, :], below[:, :, :], AX_X, ALU.add))
                if h == 0:
                    link(dve.scalar_tensor_tensor(
                        out=place[:, :, :], in0=first[:, 0, :].unsqueeze(1).broadcast_to([P, TT, EB]),
                        scalar=float(P), in1=rank, op0=ALU.mult, op1=ALU.add))
                else:
                    link(dve.tensor_scalar(first[:, 1, :], first[:, 1, :], all_0[:, 0:1], None, ALU.add))
                    link(dve.tensor_tensor(jump[:, :], first[:, 1, :], first[:, 0, :], ALU.subtract))
                    link(dve.scalar_tensor_tensor(out=jump[:, :], in0=jump[:, :], scalar=float(P),
                                                  in1=room[:, :], op0=ALU.mult, op1=ALU.subtract))
                    link(dve.tensor_tensor(moved[:, :, :], rank,
                                           room[:, :].unsqueeze(1).broadcast_to([P, TT, EB]), ALU.is_ge))
                    link(dve.tensor_tensor(moved[:, :, :], moved[:, :, :],
                                           jump[:, :].unsqueeze(1).broadcast_to([P, TT, EB]), ALU.mult))
                    link(dve.scalar_tensor_tensor(
                        out=moved[:, :, :], in0=first[:, 0, :].unsqueeze(1).broadcast_to([P, TT, EB]),
                        scalar=float(P), in1=moved[:, :, :], op0=ALU.mult, op1=ALU.add))
                    link(dve.tensor_tensor(place[:, :, :], rank, moved[:, :, :], ALU.add))
                for c in range(TOP):
                    ins = dve.tensor_tensor(product[:, c, :], hit[:, h, c, :],
                                            place[:, :, :].rearrange("p t e -> p (t e)"), ALU.mult)
                link(ins)
                link(dve.tensor_reduce(slot_f[:, :, :],
                                       product[:, :, :].rearrange("p c (t e) -> p c t e", t=TT), AX_X, ALU.add))
                dve.tensor_copy(slot[:, h, :, :], slot_f[:, :, :]).then_inc(slots_ready, 1)
                if h == 0:
                    link(dve.tensor_scalar(room[:, :], n_tiles[:, 0, :], float(P), None, ALU.mult))
                    link(dve.tensor_reduce(all_0[:, :], n_tiles[:, 0, :], AX_X, ALU.add))

            def find_experts():
                f = first[0:1, :, :].rearrange("p h e -> p (h e)").unsqueeze(1).broadcast_to(
                    [1, TILES, HALVES * EB])
                link(dve.tensor_tensor(passed[:, :, :],
                                       tile_no[0:1, :].unsqueeze(2).broadcast_to([1, TILES, HALVES * EB]), f,
                                       ALU.is_ge))
                link(dve.tensor_reduce(passed_n[:, :], passed[:, :, :], AX_X, ALU.add))
                link(dve.scalar_tensor_tensor(out=expert_f[:, :], in0=passed[:, :, EB], scalar=-float(EB),
                                              in1=passed_n[:, :], op0=ALU.mult, op1=ALU.add))
                dve.tensor_scalar(expert[:, :], expert_f[:, :], -1.0, None, ALU.add).then_inc(experts_ready, 1)

            def find_weights(h):
                dve.wait_ge(exps, TT * (h + 1))
                link(dve.tensor_reduce(lsum[:, :], lexp[:, h, :, :], AX_X, ALU.add))
                link(dve.reciprocal(lrec[:, :], lsum[:, :]))
                for c in range(TOP):
                    ins = dve.tensor_tensor(product[:, c, :], hit[:, h, c, :],
                                            lexp[:, h, :, :].rearrange("p t e -> p (t e)"), ALU.mult)
                link(ins)
                link(dve.tensor_reduce(picked_e[:, :, :],
                                       product[:, :, :].rearrange("p c (t e) -> p c t e", t=TT), AX_X, ALU.add))
                link(dve.tensor_tensor(weight[:, h, :, :], picked_e[:, :, :],
                                       lrec[:, :].unsqueeze(1).broadcast_to([P, TOP, TT]), ALU.mult))

            def add_shared(h):
                dve.wait_ge(downs, B0 + SHARED_TILES * (h + 1))
                for b in range(2 * h, 2 * h + 2):
                    dve.tensor_tensor(pair(b), acc[b][:, :], pair(b), ALU.add).then_inc(shared_added, 1)

            def weights_lo(b):
                dve.wait_ge(w_his, b + 1)
                dve.tensor_tensor(block_lo(b), w_raw[:, b % RAW, 0:block_cols(b)], f32(block_hi(b)),
                                  ALU.subtract).then_inc(w_los_dve, 1)

            def hidden_lo(n):
                dve.wait_ge(hid_his, n + 1)
                if n >= 3:
                    dve.wait_ge(downs, n - 2)
                dve.tensor_tensor(h_lo[n % 3][:, :], hb[:, n % 2, :], f32(h_hi[n % 3][:, :]),
                                  ALU.subtract).then_inc(hid_los_v, 1)

            def combine(h, b):
                dve.wait_ge(res_in[2 * h + b], 16 * TOP)
                for c in range(TOP):
                    if c == 1:
                        dve.wait_ge(combined, TOP * (2 * h + b) + 1)
                    for t in range(2 * b, 2 * b + 2):
                        rows_t = xt[:, TT * h + t, :]
                        ins = dve.scalar_tensor_tensor(out=rows_t, in0=res[c][:, TT * h + t, :],
                                                       scalar=weight[:, h, c, t:t + 1], in1=rows_t,
                                                       op0=ALU.mult, op1=ALU.add)
                    ins.then_inc(combined, 1)

            def between(n):
                for m, at in ((1, LN1B), (2, LN2A)):
                    for b in range(2):
                        if n == at["stats"] + b:
                            norm_stats(m, b)
                        if n == at["apply"] + (b if m != 2 else 0):
                            norm_apply(m, b)
                            if m == 2 and b == 1:
                                mark_rows(0)
                    if n == at["copy"]:
                        for k in range(KD):
                            turn_lo(m, k, work[2 + k])
                if n < EA - 1:
                    expert_ids(1, n + 1)
                if n == 2:
                    dve.wait_ge(g_in, 16)
                    dve.tensor_copy(g_hl[:, :, 0:EB], g_raw[:, :, :]).then_inc(g_his, 1)
                    dve.wait_ge(g_his, 1)
                    dve.tensor_tensor(g_hl[:, :, EB:2 * EB], g_raw[:, :, :], f32(g_hl[:, :, 0:EB]),
                                      ALU.subtract).then_inc(g_los, 1)
                if n == PICK_A:
                    choose(0)
                if n == SLOTS_A:
                    find_slots(0)

            for b in range(2):
                norm_stats(0, b)
            expert_ids(0, 1)
            expert_ids(0, 2)
            for b in range(2):
                norm_apply(0, b)
            expert_ids(0, 3)
            for k in range(KD):
                turn_lo(0, k, work[2 + k])
            for n in range(STEPS):
                h_in = hb[:, n % 2, :]
                if n < B0:
                    h, e = half_a(n), n % TILES_A // (FA // P)
                    dve.wait_ge(up_a, n + 1)
                    if n == 0:
                        dve.wait_ge(ids_step, EA - 1)
                    if n == TILES_A:
                        dve.wait_ge(ids_step, HALVES * (EA - 1))
                    if n >= 2:
                        dve.wait_ge(silus, n - 1)
                        dve.wait_ge(hiddens, n - 1)
                    dve.scalar_tensor_tensor(out=tm[:, n % 2, :], in0=ids[:, TH * h:TH * h + TH],
                                             scalar=float(e), in1=work[n % 2][:, :], op0=ALU.is_equal,
                                             op1=ALU.mult).then_inc(masked, 1)
                    if n - 1 in VECTOR_LO:
                        hidden_lo(n - 1)
                    between(n)
                    dve.wait_ge(silus, n + 1)
                    if n >= 2:
                        hidden_split(dve, n - 2)
                    dve.tensor_tensor(h_in, sg[:, n % 2, :], tm[:, n % 2, :], ALU.mult).then_inc(hiddens, 1)
                else:
                    if n == B0:
                        if n - 1 in VECTOR_LO:
                            hidden_lo(n - 1)
                        norm_stats(3, 0)
                    if n == B0 + 2:
                        choose(1)
                        mark_rows(1)
                    if n == B0 + 3:
                        find_slots(1)
                    dve.wait_ge(silus, n + 1)
                    dve.wait_ge(up_b, n - B0 + 1)
                    hidden_split(dve, n - 2)
                    dve.tensor_tensor(h_in, work[1][:, :], sg[:, n % 2, :], ALU.mult).then_inc(hiddens, 1)
                    if n == B0:
                        norm_stats(3, 1)
                    if n == B0 + 1:
                        for k in range(KD):
                            turn_lo(3, k, work[2 + k])
                    if n == B0 + 3:
                        find_experts()
                    if n == B0 + 4:
                        add_shared(0)
                    hidden_lo(n)
                    if n == B0:
                        for b in range(2):
                            norm_apply(3, b)
                    if n == B0 + 4:
                        weights_lo(BLOCKS - 1)

            def split_lo(dst, src, hi, done):
                dve.tensor_tensor(dst, src[:, 0:D], f32(hi), ALU.subtract).then_inc(done, 1)

            def slot_split(i):
                dve.wait_ge(slot_ins[i % SLOT_INS], 16 * (i // SLOT_INS + 1))
                dve.tensor_copy(result_row[:, i:i + 1],
                                slot_in[i % SLOT_INS][:, D:ROW].bitcast(U32)).then_inc(marks_read, 1)
                dve.wait_ge(slot_his, i + 1)
                if i >= 2:
                    dve.wait_ge(slot_up, i - 1)
                split_lo(slot_lo[i % 2], work[2 + i % 2], slot_hi[i % 2], slot_los)

            def slot_hidden(i):
                dve.wait_ge(slot_silu, i + 1)
                if i >= 2:
                    dve.wait_ge(hid_turned, i - 1)
                dve.tensor_tensor(hid_s[:, i % 2, 0:IB], work[i % 2][:, IB:UPC], act_s[:, i % 2, :],
                                  ALU.mult).then_inc(slot_hid, 1)

            def hid_split(i):
                dve.wait_ge(hidt_his, i + 1)
                if i >= 2:
                    dve.wait_ge(slot_down, i - 1)
                split_lo(hidt_lo[i % 2], acc[i % 2], hidt_hi[i % 2], hidt_los)

            dve.wait_ge(hid_los_v, len(VECTOR_LO))
            dve.memset(hid_s[:, :, IB:FB * P], 0.0).then_inc(hid_zero, 1)
            add_shared(1)
            slot_split(0)
            slot_split(1)
            for i in range(TILES + 1):
                if i < TILES:
                    slot_hidden(i)
                if i >= 1:
                    hid_split(i - 1)
                if i + 2 < TILES:
                    slot_split(i + 2)
                if i in WEIGHTS_AT:
                    find_weights(WEIGHTS_AT.index(i))
                if i == COMBINE_0:
                    dve.wait_ge(shared_added, 2 * HALVES)
                    for b in range(2):
                        combine(0, b)
            for b in range(2):
                combine(1, b)

        @block.tensor
        def _(pe):
            def turn(n, k, dst):
                if n >= 1:
                    pe.wait_ge(normed, TT * (n + 1))
                    pe.wait_ge(ht_los, KD * n - KD + k + 1)
                if n == 3:
                    pe.wait_ge(slots_ready if k == 0 else shifted, 1)
                for t in range(TT):
                    if n == 0:
                        pe.wait_ge(normed, t + 1)
                    src = hn[:, t, P * k:P * k + P] if n != 2 else rows[:, 0, t, P * k:P * k + P]
                    mm = pe.transpose(dst[:, P * t:P * t + P], src, ident)
                mm.then_inc(turned, 1)

            def up_passes(dst, hi, lo, s, h):
                cols = slice(TH * h, TH * h + TH)
                for k in range(KD):
                    for w, v in ((hi, ht_hi[s]), (hi, ht_lo[s]), (lo, ht_hi[s])):
                        mm = pe.matmul(dst[:, :], w(k), v[:, k, cols], start=(k == 0 and w is hi and v is ht_hi[s]),
                                       stop=(k == KD - 1 and w is lo))
                return mm

            def up(n):
                h, e, f = half_a(n), n % TILES_A // (FA // P), n % (FA // P)
                pe.wait_ge(c_los, e + 1)
                pe.wait_ge(ht_los, KD * (h + 1))
                if n >= 2:
                    pe.wait_ge(masked, n - 1)
                up_passes(work[n % 2], lambda k: c_hi[:, e, D * k + P * f:D * k + P * f + P],
                          lambda k: c_lo[:, e, D * k + P * f:D * k + P * f + P], 0, h).then_inc(up_a, 1)

            def up_1(n):
                h, g = half_b(n), tile_b(n)
                block_split(pe, g)
                pe.wait_ge(ht_los, KD * (2 + h + 1))
                if n == B0:
                    pe.wait_ge(masked, STEPS_A)
                else:
                    pe.wait_ge(silus, n)
                up_passes(work[0], lambda k: ws_hi[:, g, P * k:P * k + P],
                          lambda k: ws_lo[:, g, P * k:P * k + P], 1, h).then_inc(up_a, 1)

            def up_3(n):
                h, g = half_b(n), tile_b(n)
                if n > B0:
                    pe.wait_ge(hiddens, n)
                up_passes(work[1], lambda k: ws_hi[:, g, P * (KD + k):P * (KD + k) + P],
                          lambda k: ws_lo[:, g, P * (KD + k):P * (KD + k) + P], 1, h).then_inc(up_b, 1)

            def down(n):
                if n < B0:
                    h, first, last = half_a(n), n % TILES_A == 0, n % TILES_A == TILES_A - 1
                    e, f = n % TILES_A // (FA // P), n % (FA // P)
                    hi, lo = c_hi[:, e, D * f:D * f + D], c_lo[:, e, D * f:D * f + D]
                else:
                    h, g = half_b(n), tile_b(n)
                    first, last = g == 0, g == SHARED_TILES - 1
                    hi, lo = ws_hi[:, g, SHARED_COLS - D:SHARED_COLS], ws_lo[:, g, SHARED_COLS - D:SHARED_COLS]
                    if first:
                        pe.wait_ge(resid, 2 * (h + 1))
                hidden_split(pe, n)
                for t in range(TT):
                    rows, cols = slice(P * t, P * t + P), slice(D * (t % 2), D * (t % 2) + D)
                    for i, (v, w) in enumerate(((h_hi, hi), (h_hi, lo), (h_lo, hi))):
                        mm = pe.matmul(acc[2 * h + t // 2][:, cols], v[n % 3][:, rows], w,
                                       start=(first and i == 0 and t % 2 == 0), stop=(last and i == 2),
                                       skip_group_check=True)
                mm.then_inc(downs, 1)

            def gate(h):
                pe.wait_ge(g_los, 1)
                pe.wait_ge(ht_los, KD * (2 + h + 1))
                for t in range(TT):
                    rows = slice(TH * h + P * t, TH * h + P * t + P)
                    for k in range(KD):
                        for v in (ht_hi[1], ht_lo[1]):
                            mm = pe.matmul(work[3][:, 2 * EB * t:2 * EB * t + 2 * EB], v[:, k, rows], g_hl[:, k, :],
                                           start=(k == 0 and v is ht_hi[1]), stop=(k == KD - 1 and v is ht_lo[1]))
                mm.then_inc(gated, 1)

            def count(h):
                pe.wait_ge(chosens, h + 1)
                if h == 0:
                    pe.wait_ge(before_ready, 1)
                    pe.wait_ge(fills, 3)
                tiles = range(TT * h, TT * h + TT)
                for t in tiles:
                    dst = work[2][:, EB * (t - TT * h):EB * (t - TT * h) + EB]
                    pe.matmul(dst, before_b[:, :], chosen[:, t, :], start=True, stop=(t == 0))
                    for u in range(t):
                        pe.matmul(dst, ones_b[:, :], chosen[:, u, :], start=False, stop=(u == t - 1))
                dst = work[2][:, TT * EB:TT * EB + EB]
                for u in range(tiles[-1] + 1):
                    mm = pe.matmul(dst, ones_b[:, :], chosen[:, u, :], start=(u == 0), stop=(u == tiles[-1]))
                mm.then_inc(counted, 1)

            pe.wait_ge(fills, 1)
            for _ in range(WARM_UPS):
                pe.matmul(work[0][:, :], ones_b[:, :], ones_b[:, :].unsqueeze(1).broadcast_to([P, TH // P, P]),
                          start=True, stop=True)
            pe.wait_ge(cst_in, 16)
            for k in range(KD):
                turn(0, k, work[2 + k])
            for n in range(STEPS_A):
                up(n)
                if n == COUNT_A:
                    count(0)
                if n >= LAG_A:
                    down(n - LAG_A)
                for m, at in ((1, LN1B), (2, LN2A)):
                    if n == at["turn"]:
                        for k in range(KD):
                            turn(m, k, work[2 + k])
                if n == PICK_A:
                    gate(0)
            down(STEPS_A - 2)
            for n in range(B0, STEPS):
                up_1(n)
                if n == B0:
                    down(STEPS_A - 1)
                if n == B0 + 2:
                    gate(1)
                up_3(n)
                if n > B0:
                    down(n - 1)
                if n == B0 + 2:
                    count(1)
                if n == B0 + 1:
                    for k in range(KD):
                        turn(3, k, work[2 + k])
            down(STEPS - 1)

            pe.wait_ge(experts_ready, 1)
            pe.wait_ge(w_los_dve, BLOCKS - POOL_BLOCKS)
            pe.wait_ge(w_los_pool, POOL_BLOCKS)
            pe.wait_ge(hid_zero, 1)
            held = {}

            def slot_turn(i):
                pe.wait_ge(slot_ins[i % SLOT_INS], 16 * (i // SLOT_INS + 1))
                if i >= 2:
                    pe.wait_ge(slot_los, i - 1)
                for k in range(KD):
                    mm = pe.transpose(work[2 + i % 2][:, P * k:P * k + P],
                                      slot_in[i % SLOT_INS][:, P * k:P * k + P], ident)
                mm.then_inc(slot_turned, 1)

            def three(dst, n_slices, v_hi, v_lo, w_of):
                for k in range(n_slices):
                    for i, (v, w) in enumerate(((v_hi, we_hi), (v_hi, we_lo), (v_lo, we_hi))):
                        mm = pe.matmul(dst, v[:, P * k:P * k + P], w_of(w, k), start=(k == 0 and i == 0),
                                       stop=(k == n_slices - 1 and i == 2))
                return mm

            def slot_products(i):
                held[i] = pe.value_load(expert[0:1, i:i + 1], min_val=0, max_val=EB - 1)
                pe.wait_ge(slot_los, i + 1)
                if i >= 2:
                    pe.wait_ge(slot_hid, i - 1)
                three(work[i % 2][:, 0:UPC], KD, slot_hi[i % 2], slot_lo[i % 2],
                      lambda w, k: w[:, bass.ds(held[i], 1), UPC * k:UPC * k + UPC]).then_inc(slot_up, 1)

            def hid_turn(i):
                pe.wait_ge(slot_hid, i + 1)
                if i < 2:
                    pe.wait_ge(shared_added, i + 1)
                else:
                    pe.wait_ge(hidt_los, i - 1)
                for k in range(FB):
                    mm = pe.transpose(acc[i % 2][:, P * k:P * k + P], hid_s[:, i % 2, P * k:P * k + P], ident)
                mm.then_inc(hid_turned, 1)

            def slot_results(i):
                pe.wait_ge(hidt_los, i + 1)
                if i < 2:
                    pe.wait_ge(shared_added, 2 + i + 1)
                else:
                    pe.wait_ge(slot_done, i - 1)
                e = held.pop(i)
                three(acc[2 + i % 2][:, 0:D], FB, hidt_hi[i % 2], hidt_lo[i % 2],
                      lambda w, k: w[:, bass.ds(e, 1), KD * UPC + D * k:KD * UPC + D * k + D]).then_inc(slot_down, 1)

            slot_turn(0)
            slot_turn(1)
            for i in range(TILES + 2):
                if i < TILES:
                    slot_products(i)
                if 1 <= i < TILES + 1:
                    hid_turn(i - 1)
                if i + 2 < TILES:
                    slot_turn(i + 2)
                if i >= 2:
                    slot_results(i - 2)


def kernel(**inputs):
    import numpy as np
    import concourse.bacc as bacc
    from concourse.bass_utils import run_bass_kernel_spmd as run

    x = np.asarray(inputs["x"])
    tok = np.ascontiguousarray(np.asarray(inputs["itok_BxS_13_99985"]).reshape(T))
    c = np.asarray(inputs["ctx_2048"])

    def by_slices(m, slices):
        *lead, rows, n = m.shape
        return m.reshape(*lead, slices, P, n).swapaxes(-3, -2).reshape(*lead, P, slices * n)

    def padded(m, rows):
        out = np.zeros((*m.shape[:-2], rows, m.shape[-1]), m.dtype)
        out[..., :m.shape[-2], :] = m
        return out

    ctx_t = np.ascontiguousarray(by_slices(c.transpose(0, 2, 1), KD))
    a = {k: np.asarray(inputs["L0_ffn_" + k]) for k in ("gate_w", "w1", "w2", "w3", "sw1", "sw2", "sw3")}
    up_1, up_3 = (by_slices(padded(a[k], SHARED_TILES * P).reshape(SHARED_TILES, P, D).transpose(0, 2, 1), KD)
                  for k in ("sw1", "sw3"))
    down = padded(a["sw2"].T, SHARED_TILES * P).reshape(SHARED_TILES, P, D)
    w_shared = np.ascontiguousarray(np.concatenate([up_1, up_3, down], axis=2))
    up_13 = by_slices(np.concatenate([a["w1"].transpose(0, 2, 1), a["w3"].transpose(0, 2, 1)], axis=2), KD)
    down = by_slices(padded(a["w2"].transpose(0, 2, 1), FB * P), FB)
    w_expert = np.ascontiguousarray(np.concatenate([up_13, down], axis=2))
    gate_t = np.ascontiguousarray(by_slices(a["gate_w"].T, KD).reshape(P, KD, EB))

    def on_all(row):
        return np.tile(np.asarray(row, np.float32).reshape(1, -1), (P, 1))

    token = np.arange(T).reshape(HALVES * TT, P)
    consts = np.ascontiguousarray(np.concatenate([
        np.eye(P, dtype=np.float32),
        np.triu(np.ones((P, P), np.float32), 1),
        on_all(np.tile(np.arange(EB), TT)),
        on_all(np.tile(P * np.arange(EB), EB)),
        on_all(np.tril(np.ones((EB, EB)), -1)),
        on_all(np.arange(TILES)),
        np.concatenate([token, token + T]).T.astype(np.float32)], axis=1))

    nc = bacc.Bacc("TRN2", target_bir_lowering=False, num_devices=1)
    arrays, args = {}, []
    for name, v in (("x", np.ascontiguousarray(x.reshape(T, D))), ("tok", tok), ("ctx_t", ctx_t),
                    ("gate_t", gate_t), ("w_shared", w_shared), ("w_expert", w_expert), ("consts", consts)):
        arrays[name] = v
        args.append(nc.dram_tensor(name, v.shape, mybir.dt.from_np(v.dtype), kind="ExternalInput").ap())
    args.append(nc.dram_tensor("slot_rows", (TILES * P, ROW), F32, kind="Internal").ap())
    args.append(nc.dram_tensor("result_rows", (TOP * T, D), F32, kind="Internal").ap())
    args.append(nc.dram_tensor("out", (T, D), F32, kind="ExternalOutput").ap())
    build(nc, *args)
    r = run(nc, [arrays], core_ids=[0])
    return r.results[0]["out"].reshape(x.shape)
```

```python
from contextlib import ExitStack

import concourse.bass as bass
from concourse import mybir

P = 128
T, D = 1024, 256
KD = D // P
HALVES = 2
TH = T // HALVES
TT = TH // P
EA = 4
FA = 256
IDS_PER_EXPERT = 12500 // EA
EB, IB = 8, 176
SHARED = 2 * IB
SHARED_TILES = -(-SHARED // P)
SHARED_COLS = 2 * KD * P + D
FB = -(-IB // P)
TAIL = IB - P
TWICE = P // 2
assert TAIL <= TWICE and FB == 2
UPC = 2 * IB
EXPERT_COLS = KD * UPC + FB * D
BLOCKS = SHARED_TILES + EB
EPS = 1e-5
E_FLOAT = 2.718281828459045
TOP = 2
TILES_0 = TH * TOP // P + EB - 1
TILES = T * TOP // P + EB - 1
ROW = D + 1
EMPTIED = 4
SLOT_INS, SLOT_OUTS = 5, 4
NO_ROW = 1 << 20

TILES_A = EA * FA // P
STEPS_A = HALVES * TILES_A
STEPS_B = HALVES * SHARED_TILES
STEPS = STEPS_A + STEPS_B
LAG_A = 3
SPLITS = LAG_A + 1
RAW = 2

B0 = STEPS_A
LN1B = dict(stats=(-1, 0), apply=(2, 2), turn=4, copy=(5, 5))
LN2A = dict(stats=(9, 10), apply=(12, 12), turn=13, copy=(13, 13))
PICK_A, COUNT_A, SLOTS_A = 14, 15, 15
VECTOR_LO = (2, 3, 5, 7, 10, 12, 15) + tuple(range(STEPS_A, STEPS))
HI_AT = ((1, 1), (2, 2), (4, 4), (5, 6), (7, 7), (9, 10), (11, 12), (13, 13), (16, 16), (19, 19), (19, 19))
LO_AT = [2, 3, 5, 6, 7, 10, 12, 15]
POOL_BLOCKS_A = len(LO_AT)
POOL_BLOCKS = 9
WARM_UPS = 18
WARM_SLOTS = 4
IDS_AT = (5, 6, 7)
RSQRT_3 = (0, 1, 0)
WEIGHTS_AT = 8
WEIGHT_STEPS = 5

F32 = mybir.dt.float32
F32R = mybir.dt.float32r
I32 = mybir.dt.int32
U32 = mybir.dt.uint32
BF16 = mybir.dt.bfloat16
ALU = mybir.AluOpType
ACT = mybir.ActivationFunctionType
AX_X = mybir.AxisListType.X


def build(nc, x, tok, ctx_t, gate_t, w_shared, w_expert, consts, slot_rows, result_rows, out):
    x_tiles = x.rearrange("(t p) d -> p t d", p=P)
    out_tiles = out.rearrange("(t p) d -> p t d", p=P)

    with ExitStack() as ctx:
        def sb(name, shape, dt=F32):
            return ctx.enter_context(nc.sbuf_tensor(name, shape, dt))

        def bank(name):
            return ctx.enter_context(nc.psum_tensor(name, [P, 512], F32))

        def sem(name):
            return ctx.enter_context(nc.semaphore(name))

        xt = sb("xt", [P, HALVES * TT, D])
        ids = sb("ids", [P, T], BF16)
        cst = sb("cst", [P, 2 * P + TT * EB + 2 * EB * EB + TILES + TOP * HALVES * TT])
        at = 0
        views = []
        for cols in (P, P, TT * EB, EB * EB, EB * EB, TILES, TOP * HALVES * TT):
            views.append(cst[:, at:at + cols])
            at += cols
        ident, before_f, iota, starts, lower, tile_no, row_no = views
        iota = iota.rearrange("p (t e) -> p t e", t=TT)
        starts = starts.rearrange("p (e k) -> p e k", e=EB)
        lower = lower.rearrange("p (e f) -> p e f", e=EB)
        row_no = row_no.rearrange("p (r t) -> p r t", r=TOP)
        before_b = sb("before_b", [P, P], BF16)
        ones_b = sb("ones_b", [P, P], BF16)
        scratch = sb("scratch", [P, TT * TOP * ROW])
        c_raw = scratch[:, 0:EA * KD * D].rearrange("p (e n) -> p e n", e=EA)
        c_hi = sb("c_hi", [P, EA, KD * D], F32R)
        c_lo = sb("c_lo", [P, EA, KD * D], F32R)
        rows = scratch[:, :].rearrange("p (r t n) -> p r t n", r=TOP, t=TT)
        w_raw = sb("w_raw", [P, RAW, EXPERT_COLS])
        ws_hi = sb("ws_hi", [P, SHARED_TILES, SHARED_COLS], F32R)
        ws_lo = sb("ws_lo", [P, SHARED_TILES, SHARED_COLS], F32R)
        we_hi = sb("we_hi", [P, EB, EXPERT_COLS], F32R)
        we_lo = sb("we_lo", [P, EB, EXPERT_COLS], F32R)
        g_raw = sb("g_raw", [P, KD, EB])
        g_hl = sb("g_hl", [P, KD, 2 * EB], F32R)
        stat = sb("stat", [P, TT, 6])
        mv = sb("mv", [P, TT, 2])
        var_eps = sb("var_eps", [P, TT])
        rstd = sb("rstd", [P, TT])
        power = sb("power", [P, TT])
        base_e = sb("base_e", [P, TT, EB])
        hn = sb("hn", [P, TT, D])
        hn_all = hn[:, :, :].rearrange("p t d -> p (t d)")
        ids_raw = [w_raw[:, 1, 0:TH].bitcast(I32), hn_all[:, 0:TH].bitcast(I32)]
        empty = hn_all[:, TH:TH + ROW]
        ht_hi = [sb(f"ht_hi{s}", [P, KD, T], F32R) for s in range(2)]
        ht_lo = [sb(f"ht_lo{s}", [P, KD, T], F32R) for s in range(2)]
        tm = sb("tm", [P, 2, TH])
        sg = sb("sg", [P, 2, TH])
        hb = sb("hb", [P, 2, TH])
        h_hi = [sb(f"h_hi{s}", [P, TH], F32R) for s in range(SPLITS)]
        h_lo = [sb(f"h_lo{s}", [P, TH], F32R) for s in range(SPLITS)]
        logit = sb("logit", [P, TT, EB])
        lsub = sb("lsub", [P, HALVES, TT, EB])
        lexp = sb("lexp", [P, HALVES, TT, EB])
        lsum = sb("lsum", [P, TT])
        lrec = sb("lrec", [P, TT])
        top_w = sb("top_w", [P, TT, 8])
        top_i = sb("top_i", [P, TT, 8], U32)
        top_if = sb("top_if", [P, TT, TOP])
        hit = sb("hit", [P, HALVES, TOP, TT * EB])
        chosen = sb("chosen", [P, HALVES * TT, EB], BF16)
        chosen_0 = sb("chosen_0", [P, EB], BF16)
        product = sb("product", [P, TOP, TT * EB])
        picked_e = sb("picked_e", [P, TOP, TT])
        weight = sb("weight", [P, HALVES, TOP, TT])
        over = sb("over", [P, EB, EB])
        n_tiles = sb("n_tiles", [P, HALVES, EB])
        first = sb("first", [P, HALVES, EB])
        below = sb("below", [P, EB, EB])
        room = sb("room", [P, EB])
        ends = starts
        back = sb("back", [P, EB])
        jump = sb("jump", [P, EB])
        all_0 = sb("all_0", [P, 1])
        place = sb("place", [P, TT, EB])
        moved = sb("moved", [P, TT, EB])
        slot_f = sb("slot_f", [P, TOP, TT])
        slot = sb("slot", [P, HALVES, TOP, TT], U32)
        passed = tm[0:1, 0, 0:TILES * HALVES * EB].rearrange("p (i f) -> p i f", i=TILES)
        passed_n = sb("passed_n", [1, TILES])
        expert_f = sb("expert_f", [1, TILES])
        expert = sb("expert", [1, TILES], I32)
        slot_in = [tm[:, :, :].rearrange("p a n -> p (a n)")[:, ROW * a:ROW * a + ROW] for a in range(3)]
        slot_in += [sg[:, a, IB:IB + ROW] for a in range(2)]
        act_s = sg[:, :, 0:IB]
        hid_s = hb[:, :, 0:FB * P]
        result_row = sb("result_row", [P, TILES], U32)
        slot_out = hn
        slot_hi, slot_lo, hidt_hi, hidt_lo = (
            [v[:, k, D * a:D * a + D] for a in range(2)] for v in (ht_hi[0], ht_lo[0]) for k in range(KD))
        res = [scratch[:, 0:HALVES * TT * D].rearrange("p (t d) -> p t d", d=D),
               w_raw[:, :, :].rearrange("p a n -> p (a n)")[:, 0:HALVES * TT * D].rearrange("p (t d) -> p t d", d=D)]

        work = [bank(f"work{b}") for b in range(4)]
        acc = [bank(f"acc{b}") for b in range(4)]

        x_in = [sem(f"x_in{i}") for i in range(2 * HALVES)]
        ids_in = [sem(f"ids_in{h}") for h in range(HALVES)]
        cst_in, g_in = sem("cst_in"), sem("g_in")
        c_in = [sem(f"c_in{e}") for e in range(EA)]
        w_in = [sem(f"w_in{s}") for s in range(RAW)]
        empty_ready = sem("empty_ready")
        emptied = sem("emptied")
        rows_out = sem("rows_out")
        slot_ins = [sem(f"slot_ins{a}") for a in range(SLOT_INS)]
        results_out = [sem(f"results_out{a}") for a in range(SLOT_OUTS)]
        res_in = [sem(f"res_in{i}") for i in range(HALVES * TT)]
        out_done = sem("out_done")
        fills = sem("fills")
        resid = sem("resid")
        doubled = sem("doubled")
        stats, moments, vars_ready = sem("stats"), sem("moments"), sem("vars_ready")
        rstds, normed = sem("rstds"), sem("normed")
        turned = sem("turned")
        ht_his, ht_los = sem("ht_his"), sem("ht_los")
        ids_step = sem("ids_step")
        c_his, c_los, w_his = sem("c_his"), sem("c_los"), sem("w_his")
        w_low_step = sem("w_low_step")
        w_los_pool, w_los_dve = sem("w_los_pool"), sem("w_los_dve")
        g_his, g_los, before_ready = sem("g_his"), sem("g_los"), sem("before_ready")
        up_a = sem("up_a")
        up_b = sem("up_b")
        masked = sem("masked")
        silus, hiddens = sem("silus"), sem("hiddens")
        hid_his = sem("hid_his")
        hid_los_v, hid_los_p = sem("hid_los_v"), sem("hid_los_p")
        downs = sem("downs")
        gated, counted = sem("gated"), sem("counted")
        link_done = sem("link_done")
        shifted, exps = sem("shifted"), sem("exps")
        chosens, slots_ready, marked = sem("chosens"), sem("slots_ready"), sem("marked")
        experts_ready = sem("experts_ready")
        weight_link = sem("weight_link")
        shared_added = sem("shared_added")
        marks_read = sem("marks_read")
        slot_turned, slot_his, slot_los = sem("slot_turned"), sem("slot_his"), sem("slot_los")
        slot_up, slot_silu, slot_hid = sem("slot_up"), sem("slot_silu"), sem("slot_hid")
        hid_zero = sem("hid_zero")
        hid_turned, hidt_his, hidt_los = sem("hid_turned"), sem("hidt_his"), sem("hidt_los")
        slot_down, slot_done = sem("slot_down"), sem("slot_done")
        combined = sem("combined")
        results = sem("results")

        block = ctx.enter_context(nc.Block())

        def half_a(n):
            return n // TILES_A

        def half_b(n):
            return (n - B0) // SHARED_TILES

        def tile_b(n):
            return (n - B0) % SHARED_TILES

        def block_cols(b):
            return SHARED_COLS if b < SHARED_TILES else EXPERT_COLS

        def block_hi(b):
            return ws_hi[:, b, :] if b < SHARED_TILES else we_hi[:, b - SHARED_TILES, :]

        def block_lo(b):
            return ws_lo[:, b, :] if b < SHARED_TILES else we_lo[:, b - SHARED_TILES, :]

        def twice(rows):
            return rows[TWICE:P, EXPERT_COLS - D:EXPERT_COLS]

        def block_split(eng, b):
            if b < POOL_BLOCKS:
                eng.wait_ge(w_los_pool, b + 1)
            else:
                eng.wait_ge(w_los_dve, b - POOL_BLOCKS + 1)

        def pair(i):
            return xt[:, 2 * i:2 * i + 2, :].rearrange("p t d -> p (t d)")

        def hidden_split(eng, n):
            if n in VECTOR_LO:
                eng.wait_ge(hid_los_v, VECTOR_LO.index(n) + 1)
            else:
                eng.wait_ge(hid_los_p, n + 1 - sum(v < n for v in VECTOR_LO))

        def f32(ap):
            return ap.bitcast(F32)

        def results_stand(eng, h):
            last = (TILES_0 if h == 0 else TILES) - 1
            for a in range(SLOT_OUTS):
                i = last - (last - a) % SLOT_OUTS
                eng.wait_ge(results_out[a], 16 * (i // SLOT_OUTS + 1))

        def read_results(eng, t, c):
            eng.dma_start(res[c][:, t, :], result_rows[T * c + P * t:T * c + P * t + P, :]).then_inc(res_in[t], 16)

        @block.sync
        def _(sp):
            sp.dma_start(xt[:, 0:2, :], x_tiles[:, 0:2, :]).then_inc(x_in[0], 16)
            sp.dma_start(ids_raw[0], tok[0:TH].partition_broadcast(P)).then_inc(ids_in[0], 16)
            sp.dma_start(c_raw[:, 0, :], ctx_t[0]).then_inc(c_in[0], 16)
            for i in range(2, 4):
                sp.dma_start(xt[:, 2 * i:2 * i + 2, :], x_tiles[:, 2 * i:2 * i + 2, :]).then_inc(x_in[i], 16)
            for e in range(1, EA):
                sp.dma_start(c_raw[:, e, :], ctx_t[e]).then_inc(c_in[e], 16)
            for b in range(BLOCKS):
                if b == 1:
                    sp.wait_ge(ids_step, EA - 1)
                if b >= RAW:
                    block_split(sp, b - RAW)
                src = w_shared[b] if b < SHARED_TILES else w_expert[b - SHARED_TILES]
                sp.dma_start(w_raw[:, b % RAW, 0:block_cols(b)], src).then_inc(w_in[b % RAW], 16)
                i = EMPTIED * (b - SHARED_TILES)
                j = min(i + EMPTIED, TILES)
                if i == 0:
                    sp.wait_ge(turned, 2 * KD)
                    sp.dma_start(ids_raw[1], tok[TH:T].partition_broadcast(P)).then_inc(ids_in[1], 16)
                    sp.wait_ge(empty_ready, 2)
                if 0 <= i < j:
                    sp.dma_start(slot_rows[P * i:P * j, :].rearrange("(i p) n -> p i n", p=P),
                                 empty[:, :].unsqueeze(1).broadcast_to([P, j - i, ROW])).then_inc(emptied, 16)
            sp.wait_ge(rows_out, 16 * HALVES * TOP * TT)

            def read_slots(i):
                if i == 0:
                    sp.wait_ge(experts_ready, 1)
                if i == 3:
                    sp.wait_ge(hiddens, STEPS)
                if i >= SLOT_INS:
                    sp.wait_ge(slot_turned, i - SLOT_INS + 1)
                    sp.wait_ge(marks_read, i - SLOT_INS + 1)
                sp.dma_start(slot_in[i % SLOT_INS], slot_rows[P * i:P * i + P, :]).then_inc(
                    slot_ins[i % SLOT_INS], 16)

            for i in range(TILES):
                read_slots(i)
            results_stand(sp, 0)
            for t in range(TT):
                for c in range(TOP):
                    read_results(sp, t, c)
            results_stand(sp, 1)
            for t in range(TT, HALVES * TT):
                read_results(sp, t, 0)
            sp.wait_ge(combined, TOP * TT)
            sp.dma_start(out_tiles[:, 0:TT, :], xt[:, 0:TT, :]).then_inc(out_done, 16)
            sp.wait_ge(out_done, 16 * (1 + TT))

        @block.gpsimd
        def _(pool):
            pool.memset(ones_b[:, :], 1.0).then_inc(fills, 1)
            pool.memset(power[:, :], -0.5).then_inc(fills, 1)
            pool.memset(base_e[:, :, :], E_FLOAT).then_inc(fills, 1)
            pool.wait_ge(fills, 3)

            def rsqrt(n):
                pool.wait_ge(vars_ready, n + 1)
                if n >= 1:
                    pool.wait_ge(normed, TT * n)
                pool.tensor_tensor(rstd[:, :], var_eps[:, :], power[:, :], ALU.pow).then_inc(rstds, 1)

            def exponent(h, t):
                pool.wait_ge(shifted, h + 1)
                pool.tensor_tensor(lexp[:, h, t, :], base_e[:, t, :], lsub[:, h, t, :], ALU.pow).then_inc(exps, 1)

            def weights_lo(b):
                pool.wait_ge(w_his, 2 * (b + 1))
                cols = block_cols(b)
                ins = pool.tensor_tensor(block_lo(b), w_raw[:, b % RAW, 0:cols], f32(block_hi(b)), ALU.subtract)
                if b >= SHARED_TILES:
                    ins.then_inc(w_low_step, 1)
                    if b >= POOL_BLOCKS_A:
                        pool.wait_ge(rows_out, 16 * TOP * TT)
                    pool.wait_ge(w_low_step, b - SHARED_TILES + 1)
                    ins = pool.tensor_tensor(twice(block_hi(b)), twice(w_raw[:, b % RAW, :]),
                                             f32(twice(block_hi(b))), ALU.subtract)
                ins.then_inc(w_los_pool, 1)
                if b >= SHARED_TILES:
                    pool.wait_ge(w_los_pool, b + 1)

            def scatter_rows(h):
                if h == 0:
                    pool.wait_ge(emptied, 16 * -(-TILES // EMPTIED))
                pool.wait_ge(slots_ready, h + 1)
                pool.wait_ge(marked, h + 1)
                for c in range(TOP):
                    if h == 0 and c == 0:
                        pool.wait_ge(normed, TT * 3)
                    else:
                        pool.wait_ge(doubled, 1 if h == 0 else c + 2)
                    for t in range(TT):
                        pool.indirect_dma_start(slot_rows, bass.IndirectOffsetOnAxis(slot[:, h, c, t:t + 1], 0),
                                                rows[:, c, t, :], None).then_inc(rows_out, 16)
                        if (h, c, t) == RSQRT_3:
                            rsqrt(3)

            def scatter_results(i):
                pool.wait_ge(slot_done, i + 1)
                pool.indirect_dma_start(result_rows, bass.IndirectOffsetOnAxis(result_row[:, i:i + 1], 0),
                                        slot_out[:, i % SLOT_OUTS, :], None, bounds_check=TOP * T - 1,
                                        oob_is_err=False).then_inc(results_out[i % SLOT_OUTS], 16)

            rsqrt(0)
            for e in range(EA):
                pool.wait_ge(c_his, e + 1)
                pool.tensor_tensor(c_lo[:, e, :], c_raw[:, e, :], f32(c_hi[:, e, :]),
                                   ALU.subtract).then_inc(c_los, 1)
            rsqrt(1)
            for n in range(STEPS_A):
                if n not in VECTOR_LO:
                    pool.wait_ge(hid_his, n + 1)
                    if n >= SPLITS:
                        pool.wait_ge(downs, n - SPLITS + 1)
                    pool.tensor_tensor(h_lo[n % SPLITS][:, :], hb[:, n % 2, :], f32(h_hi[n % SPLITS][:, :]),
                                       ALU.subtract).then_inc(hid_los_p, 1)
                if n == LN1B["turn"]:
                    pool.wait_ge(turned, 2 * KD)
                    pool.memset(empty[:, 0:D], 0.0).then_inc(empty_ready, 1)
                    pool.memset(empty[:, D:ROW].bitcast(U32), NO_ROW).then_inc(empty_ready, 1)
                if n == LN2A["stats"][1]:
                    rsqrt(2)
                if n in LO_AT:
                    weights_lo(LO_AT.index(n))
            scatter_rows(0)
            for b in range(POOL_BLOCKS_A, POOL_BLOCKS):
                weights_lo(b)
            scatter_rows(1)
            for i in range(TILES):
                if i < HALVES * TT:
                    exponent(i // TT, i % TT)
                scatter_results(i)

        @block.scalar
        def _(act):
            act.dma_start(xt[:, 2:4, :], x_tiles[:, 2:4, :]).then_inc(x_in[1], 16)
            act.dma_start(cst[:, :], consts).then_inc(cst_in, 16)
            act.dma_start(g_raw[:, :, :], gate_t).then_inc(g_in, 16)
            nc.scalar.preload_act_table(ACT.Silu)

            def ctx_hi(e):
                act.wait_ge(c_in[e], 16)
                act.activation(c_hi[:, e, :], c_raw[:, e, :], ACT.Copy).then_inc(c_his, 1)

            def turn_hi(n, k, src):
                s, h = n // 2, n % 2
                act.wait_ge(turned, KD * n + k + 1)
                act.activation(ht_hi[s][:, k, TH * h:TH * h + TH], src[:, :], ACT.Copy).then_inc(ht_his, 1)

            def weights_hi(b, part):
                if part == 0:
                    act.wait_ge(w_in[b % RAW], 16 * (b // RAW + 1))
                cols = slice(part * block_cols(b) // 2, (part + 1) * block_cols(b) // 2)
                act.activation(block_hi(b)[:, cols], w_raw[:, b % RAW, cols], ACT.Copy).then_inc(w_his, 1)

            def double(h):
                act.wait_ge(normed, TT * (3 + h))
                if h == 0:
                    act.activation(rows[:, 1, :, 0:D], rows[:, 0, :, 0:D], ACT.Copy).then_inc(doubled, 1)
                    return
                act.wait_ge(rows_out, 16 * TOP * TT)
                for c in range(TOP):
                    act.activation(rows[:, c, :, 0:D], hn[:, :, :], ACT.Copy).then_inc(doubled, 1)

            ctx_hi(0)
            for k in range(KD):
                turn_hi(0, k, work[2 + k])
            for e in range(1, EA):
                ctx_hi(e)
            act.wait_ge(cst_in, 16)
            act.activation(before_b[:, :], before_f, ACT.Copy).then_inc(before_ready, 1)
            for n in range(STEPS):
                if n < B0:
                    act.wait_ge(masked, n + 1)
                    src = tm[:, n % 2, :]
                else:
                    act.wait_ge(up_a, n + 1)
                    src = work[0][:, :]
                if n >= 2:
                    act.wait_ge(hiddens, n - 1)
                act.activation(sg[:, n % 2, :], src, ACT.Silu).then_inc(silus, 1)
                for m, at in ((1, LN1B), (2, LN2A)):
                    for k in range(KD):
                        if n == at["copy"][k]:
                            turn_hi(m, k, work[2 + k])
                if n == B0 + 1:
                    for k in range(KD):
                        turn_hi(3, k, work[2 + k])
                act.wait_ge(hiddens, n + 1)
                if n >= SPLITS:
                    act.wait_ge(downs, n - SPLITS + 1)
                act.activation(h_hi[n % SPLITS][:, :], hb[:, n % 2, :], ACT.Copy).then_inc(hid_his, 1)
                for b, steps in enumerate(HI_AT):
                    for part, step in enumerate(steps):
                        if n == step:
                            weights_hi(b, part)
                if n == LN2A["turn"] + 1:
                    double(0)
                if n == B0 + 2:
                    double(1)

            def split_hi(dst, src, done):
                act.activation(dst, src[:, 0:D], ACT.Copy).then_inc(done, 1)

            def slot_copy(i):
                act.wait_ge(slot_turned, i + 1)
                if i >= 2:
                    act.wait_ge(slot_up, i - 1)
                split_hi(slot_hi[i % 2], work[2 + i % 2], slot_his)

            def slot_gate(i):
                act.wait_ge(slot_up, i + 1)
                if i >= 2:
                    act.wait_ge(slot_hid, i - 1)
                act.activation(act_s[:, i % 2, :], work[i % 2][:, 0:IB], ACT.Silu).then_inc(slot_silu, 1)

            def hid_copy(i):
                act.wait_ge(hid_turned, i + 1)
                if i >= 2:
                    act.wait_ge(slot_down, i - 1)
                split_hi(hidt_hi[i % 2], acc[i % 2], hidt_his)

            def slot_store(i):
                act.wait_ge(slot_down, i + 1)
                if i >= SLOT_OUTS:
                    act.wait_ge(results_out[i % SLOT_OUTS], 16 * (i // SLOT_OUTS))
                act.activation(slot_out[:, i % SLOT_OUTS, :], acc[2 + i % 2][:, 0:D], ACT.Copy).then_inc(slot_done, 1)

            slot_copy(0)
            slot_copy(1)
            for i in range(TILES + 2):
                if i < TILES:
                    slot_gate(i)
                if 1 <= i < TILES + 1:
                    hid_copy(i - 1)
                if i + 2 < TILES:
                    slot_copy(i + 2)
                if i >= 2:
                    slot_store(i - 2)
            results_stand(act, 1)
            for t in range(TT, HALVES * TT):
                read_results(act, t, 1)
            for t in range(TT, HALVES * TT):
                act.wait_ge(combined, 2 * TOP * (t // 2) + TOP + t % 2 + 1)
                act.dma_start(out_tiles[:, t, :], xt[:, t, :]).then_inc(out_done, 16)

        @block.vector
        def _(dve):
            def norm_stats(n, b):
                h = n % 2
                if n < 2:
                    dve.wait_ge(x_in[2 * h + b], 16)
                else:
                    dve.wait_ge(downs, TILES_A * (h + 1))
                    rows = xt[:, TT * h + 2 * b:TT * h + 2 * b + 2, :].rearrange("p t d -> p (t d)")
                    dve.tensor_tensor(rows, acc[2 * h + b][:, :], rows, ALU.add).then_inc(resid, 1)
                    dve.wait_ge(resid, 2 * h + b + 1)
                for t in range(2 * b, 2 * b + 2):
                    dve.bn_stats(stat[:, t, :], xt[:, TT * h + t, :]).then_inc(stats, 1)
                for t in range(2 * b, 2 * b + 2):
                    dve.wait_ge(stats, TT * n + t + 1)
                    dve.bn_aggr(mv[:, t, :], stat[:, t, :]).then_inc(moments, 1)
                if b == 1:
                    dve.wait_ge(moments, TT * (n + 1))
                    dve.tensor_scalar(var_eps[:, :], mv[:, :, 1], EPS, None, ALU.add).then_inc(vars_ready, 1)

            def norm_apply(n, b):
                h = n % 2
                dve.wait_ge(rstds, n + 1)
                if n == 1:
                    dve.wait_ge(turned, KD)
                if n == 3 and b == 0:
                    dve.wait_ge(emptied, 16 * -(-TILES // EMPTIED))
                    dve.wait_ge(ids_step, HALVES * (EA - 1))
                if n == 2:
                    dve.wait_ge(c_los, EA)
                for t in range(2 * b, 2 * b + 2):
                    dst = hn[:, t, :] if n != 2 else rows[:, 0, t, 0:D]
                    dve.tensor_scalar(dst, xt[:, TT * h + t, :], mv[:, t, 0:1], rstd[:, t:t + 1],
                                      ALU.subtract, ALU.mult).then_inc(normed, 1)

            def mark_rows(h):
                if h == 0:
                    dve.wait_ge(cst_in, 16)
                else:
                    dve.wait_ge(rows_out, 16 * TOP * TT)
                dve.tensor_copy(rows[:, :, :, D:ROW].bitcast(U32),
                                row_no[:, :, TT * h:TT * h + TT].unsqueeze(3)).then_inc(marked, 1)

            def turn_lo(n, k, src):
                s, h = n // 2, n % 2
                dve.wait_ge(ht_his, KD * n + k + 1)
                dve.tensor_tensor(ht_lo[s][:, k, TH * h:TH * h + TH], src[:, :],
                                  f32(ht_hi[s][:, k, TH * h:TH * h + TH]), ALU.subtract).then_inc(ht_los, 1)

            def expert_ids(h, e):
                cols = slice(TH * h, TH * h + TH)
                if e == 1:
                    dve.wait_ge(ids_in[h], 16)
                    dve.tensor_scalar(ids[:, cols], ids_raw[h][:, :], float(IDS_PER_EXPERT), None,
                                      ALU.is_ge).then_inc(ids_step, 1)
                    return
                dve.wait_ge(ids_step, (EA - 1) * h + e - 1)
                dve.scalar_tensor_tensor(out=ids[:, cols], in0=ids_raw[h][:, :], scalar=float(e * IDS_PER_EXPERT),
                                         in1=ids[:, cols], op0=ALU.is_ge, op1=ALU.add).then_inc(ids_step, 1)

            links = [0]

            def link(ins):
                links[0] += 1
                ins.then_inc(link_done, 1)
                dve.wait_ge(link_done, links[0])

            def over_experts(ap):
                return ap.unsqueeze(2).broadcast_to([P, TT, EB])

            def choose(h):
                dve.wait_ge(gated, h + 1)
                link(dve.tensor_reduce(
                    logit[:, :, :], work[2][:, 0:TT * 2 * EB].rearrange("p (t s e) -> p t e s", t=TT, s=2),
                    AX_X, ALU.add))
                for t in range(TT):
                    ins = dve.max(top_w[:, t, :], logit[:, t, :])
                link(ins)
                for t in range(TT):
                    ins = dve.max_index(top_i[:, t, :], top_w[:, t, :], logit[:, t, :])
                link(ins)
                link(dve.tensor_copy(top_if[:, :, :], top_i[:, :, 0:TOP]))
                for c in range(TOP):
                    ins = dve.tensor_tensor(hit[:, h, c, :].rearrange("p (t e) -> p t e", t=TT), iota,
                                            over_experts(top_if[:, :, c]), ALU.is_equal)
                link(ins)
                dve.tensor_tensor(chosen[:, TT * h:TT * h + TT, :].rearrange("p t e -> p (t e)"),
                                  hit[:, h, 0, :], hit[:, h, 1, :], ALU.add).then_inc(chosens, 1)
                dve.tensor_tensor(lsub[:, h, :, :], logit[:, :, :], over_experts(top_w[:, :, 0]),
                                  ALU.subtract).then_inc(shifted, 1)

            def each_expert(ap):
                return ap.unsqueeze(1).broadcast_to([P, TT, EB])

            def find_slots(h):
                dve.wait_ge(counted, h + 1)
                rank = work[2][:, 0:TT * EB].rearrange("p (t e) -> p t e", t=TT)
                count = work[2][:, TT * EB:TT * EB + EB].unsqueeze(2).broadcast_to([P, EB, EB])
                link(dve.tensor_tensor(over[:, :, :], count, starts if h == 0 else ends, ALU.is_gt))
                link(dve.tensor_reduce(n_tiles[:, h, :], over[:, :, :], AX_X, ALU.add))
                ins = dve.tensor_tensor(below[:, :, :], lower,
                                        n_tiles[:, h, :].unsqueeze(1).broadcast_to([P, EB, EB]), ALU.mult)
                if h == 1:
                    dve.scalar_tensor_tensor(out=place[:, :, :], in0=each_expert(first[:, 0, :]), scalar=float(P),
                                             in1=rank, op0=ALU.mult, op1=ALU.add)
                    ins = dve.tensor_tensor(moved[:, :, :], rank, each_expert(room[:, :]), ALU.is_ge)
                link(ins)
                link(dve.tensor_reduce(first[:, h, :], below[:, :, :], AX_X, ALU.add))
                if h == 0:
                    link(dve.scalar_tensor_tensor(
                        out=place[:, :, :], in0=each_expert(first[:, 0, :]), scalar=float(P), in1=rank,
                        op0=ALU.mult, op1=ALU.add))
                else:
                    link(dve.scalar_tensor_tensor(out=jump[:, :], in0=first[:, 1, :], scalar=float(P),
                                                  in1=back[:, :], op0=ALU.mult, op1=ALU.add))
                    link(dve.tensor_tensor(moved[:, :, :], moved[:, :, :], each_expert(jump[:, :]), ALU.mult))
                    link(dve.tensor_tensor(place[:, :, :], place[:, :, :], moved[:, :, :], ALU.add))
                for c in range(TOP):
                    ins = dve.tensor_tensor(product[:, c, :], hit[:, h, c, :],
                                            place[:, :, :].rearrange("p t e -> p (t e)"), ALU.mult)
                link(ins)
                link(dve.tensor_reduce(slot_f[:, :, :],
                                       product[:, :, :].rearrange("p c (t e) -> p c t e", t=TT), AX_X, ALU.add))
                dve.tensor_copy(slot[:, h, :, :], slot_f[:, :, :]).then_inc(slots_ready, 1)

            def look_ahead():
                dve.tensor_reduce(all_0[:, :], n_tiles[:, 0, :], AX_X, ALU.add)
                dve.tensor_reduce(moved[:, 0, :], chosen[:, 0:TT, :].rearrange("p t e -> p e t"), AX_X, ALU.add)
                link(dve.tensor_scalar(room[:, :], n_tiles[:, 0, :], float(P), None, ALU.mult))
                dve.tensor_copy(chosen_0[:, :], moved[:, 0, :])
                dve.tensor_tensor(ends, starts, room[:, :].unsqueeze(2).broadcast_to([P, EB, EB]), ALU.add)
                link(dve.tensor_scalar(back[:, :], first[:, 0, :], all_0[:, 0:1], -float(P), ALU.subtract, ALU.mult))
                link(dve.tensor_tensor(back[:, :], back[:, :], room[:, :], ALU.subtract))

            def find_experts():
                link(dve.tensor_scalar(first[:, 1, :], first[:, 1, :], all_0[:, 0:1], None, ALU.add))
                f = first[0:1, :, :].rearrange("p h e -> p (h e)").unsqueeze(1).broadcast_to(
                    [1, TILES, HALVES * EB])
                link(dve.tensor_tensor(passed[:, :, :],
                                       tile_no[0:1, :].unsqueeze(2).broadcast_to([1, TILES, HALVES * EB]), f,
                                       ALU.is_ge))
                link(dve.tensor_reduce(passed_n[:, :], passed[:, :, :], AX_X, ALU.add))
                link(dve.scalar_tensor_tensor(out=expert_f[:, :], in0=passed[:, :, EB], scalar=-float(EB),
                                              in1=passed_n[:, :], op0=ALU.mult, op1=ALU.add))
                dve.tensor_scalar(expert[:, :], expert_f[:, :], -1.0, None, ALU.add).then_inc(experts_ready, 1)

            def find_weights(h, step):
                if step == 0:
                    dve.wait_ge(exps, TT * (h + 1))
                    dve.tensor_reduce(lsum[:, :], lexp[:, h, :, :], AX_X, ALU.add).then_inc(weight_link, 1)
                elif step == 1:
                    for c in range(TOP):
                        ins = dve.tensor_tensor(product[:, c, :], hit[:, h, c, :],
                                                lexp[:, h, :, :].rearrange("p t e -> p (t e)"), ALU.mult)
                    ins.then_inc(weight_link, 1)
                elif step == 2:
                    dve.wait_ge(weight_link, WEIGHT_STEPS * h + 1)
                    dve.reciprocal(lrec[:, :], lsum[:, :]).then_inc(weight_link, 1)
                elif step == 3:
                    dve.wait_ge(weight_link, WEIGHT_STEPS * h + 2)
                    dve.tensor_reduce(picked_e[:, :, :], product[:, :, :].rearrange("p c (t e) -> p c t e", t=TT),
                                      AX_X, ALU.add).then_inc(weight_link, 1)
                else:
                    dve.wait_ge(weight_link, WEIGHT_STEPS * h + 4)
                    dve.tensor_tensor(weight[:, h, :, :], picked_e[:, :, :],
                                      lrec[:, :].unsqueeze(1).broadcast_to([P, TOP, TT]),
                                      ALU.mult).then_inc(weight_link, 1)

            def add_shared(h):
                dve.wait_ge(downs, B0 + SHARED_TILES * (h + 1))
                for b in range(2 * h, 2 * h + 2):
                    dve.tensor_tensor(pair(b), acc[b][:, :], pair(b), ALU.add).then_inc(shared_added, 1)

            def weights_lo(b):
                dve.wait_ge(w_his, 2 * (b + 1))
                link(dve.tensor_tensor(block_lo(b), w_raw[:, b % RAW, 0:block_cols(b)], f32(block_hi(b)),
                                       ALU.subtract))
                dve.tensor_tensor(twice(block_hi(b)), twice(w_raw[:, b % RAW, :]), f32(twice(block_hi(b))),
                                  ALU.subtract).then_inc(w_los_dve, 1)

            def hidden_lo(n):
                dve.wait_ge(hid_his, n + 1)
                if n >= SPLITS:
                    dve.wait_ge(downs, n - SPLITS + 1)
                dve.tensor_tensor(h_lo[n % SPLITS][:, :], hb[:, n % 2, :], f32(h_hi[n % SPLITS][:, :]),
                                  ALU.subtract).then_inc(hid_los_v, 1)

            def combine(b):
                for c in range(TOP):
                    for t in (2 * b, 2 * b + 1):
                        if c == 0:
                            dve.wait_ge(res_in[t], 16 * TOP)
                        else:
                            dve.wait_ge(combined, 2 * TOP * b + 1 + t % 2)
                        dve.scalar_tensor_tensor(out=xt[:, t, :], in0=res[c][:, t, :],
                                                 scalar=weight[:, t // TT, c, t % TT:t % TT + 1], in1=xt[:, t, :],
                                                 op0=ALU.mult, op1=ALU.add).then_inc(combined, 1)

            def between(n):
                for m, at in ((1, LN1B), (2, LN2A)):
                    for b in range(2):
                        if n == at["stats"][b]:
                            norm_stats(m, b)
                        if n == at["apply"][b]:
                            norm_apply(m, b)
                            if m == 2 and b == 1:
                                mark_rows(0)
                    for k in range(KD):
                        if n == at["copy"][k]:
                            turn_lo(m, k, work[2 + k])
                if n in IDS_AT:
                    expert_ids(1, IDS_AT.index(n) + 1)
                if n == 2:
                    dve.wait_ge(g_in, 16)
                    dve.tensor_copy(g_hl[:, :, 0:EB], g_raw[:, :, :]).then_inc(g_his, 1)
                    dve.wait_ge(g_his, 1)
                    dve.tensor_tensor(g_hl[:, :, EB:2 * EB], g_raw[:, :, :], f32(g_hl[:, :, 0:EB]),
                                      ALU.subtract).then_inc(g_los, 1)
                if n == PICK_A:
                    choose(0)
                if n == SLOTS_A:
                    find_slots(0)
                    look_ahead()

            for b in range(2):
                norm_stats(0, b)
            expert_ids(0, 1)
            expert_ids(0, 2)
            for b in range(2):
                norm_apply(0, b)
            expert_ids(0, 3)
            for k in range(KD):
                turn_lo(0, k, work[2 + k])
            norm_stats(1, 0)
            for n in range(STEPS):
                h_in = hb[:, n % 2, :]
                if n < B0:
                    h, e = half_a(n), n % TILES_A // (FA // P)
                    dve.wait_ge(up_a, n + 1)
                    if n == 0:
                        dve.wait_ge(ids_step, EA - 1)
                    if n == TILES_A:
                        dve.wait_ge(ids_step, HALVES * (EA - 1))
                    if n >= 2:
                        dve.wait_ge(silus, n - 1)
                        dve.wait_ge(hiddens, n - 1)
                    dve.scalar_tensor_tensor(out=tm[:, n % 2, :], in0=ids[:, TH * h:TH * h + TH],
                                             scalar=float(e), in1=work[n % 2][:, :], op0=ALU.is_equal,
                                             op1=ALU.mult).then_inc(masked, 1)
                    if n - 1 in VECTOR_LO:
                        hidden_lo(n - 1)
                    between(n)
                    dve.wait_ge(silus, n + 1)
                    if n >= 2:
                        hidden_split(dve, n - 2)
                    dve.tensor_tensor(h_in, sg[:, n % 2, :], tm[:, n % 2, :], ALU.mult).then_inc(hiddens, 1)
                else:
                    if n == B0:
                        if n - 1 in VECTOR_LO:
                            hidden_lo(n - 1)
                        norm_stats(3, 0)
                    if n == B0 + 2:
                        choose(1)
                        mark_rows(1)
                    if n == B0 + 3:
                        find_slots(1)
                        hidden_lo(n - 1)
                    dve.wait_ge(silus, n + 1)
                    dve.wait_ge(up_b, n - B0 + 1)
                    hidden_split(dve, n - 2)
                    dve.tensor_tensor(h_in, work[1][:, :], sg[:, n % 2, :], ALU.mult).then_inc(hiddens, 1)
                    if n == B0:
                        norm_stats(3, 1)
                    if n == B0 + 1:
                        for k in range(KD):
                            turn_lo(3, k, work[2 + k])
                    if n == B0 + 3:
                        find_experts()
                    if n == B0 + 4:
                        weights_lo(BLOCKS - 1)
                    if n != B0 + 2:
                        hidden_lo(n)
                    if n == B0:
                        for b in range(2):
                            norm_apply(3, b)
                    if n == B0 + 3:
                        weights_lo(BLOCKS - 2)

            def split_lo(dst, src, hi, done):
                dve.tensor_tensor(dst, src[:, 0:D], f32(hi), ALU.subtract).then_inc(done, 1)

            def slot_split(i):
                dve.wait_ge(slot_ins[i % SLOT_INS], 16 * (i // SLOT_INS + 1))
                dve.tensor_copy(result_row[:, i:i + 1],
                                slot_in[i % SLOT_INS][:, D:ROW].bitcast(U32)).then_inc(marks_read, 1)
                dve.wait_ge(slot_his, i + 1)
                if i >= 2:
                    dve.wait_ge(slot_up, i - 1)
                split_lo(slot_lo[i % 2], work[2 + i % 2], slot_hi[i % 2], slot_los)

            def slot_hidden(i):
                dve.wait_ge(slot_silu, i + 1)
                if i >= 2:
                    dve.wait_ge(hid_turned, i - 1)
                dve.tensor_tensor(hid_s[:, i % 2, 0:IB], work[i % 2][:, IB:UPC], act_s[:, i % 2, :],
                                  ALU.mult)
                dve.tensor_tensor(hid_s[:, i % 2, P + TWICE:P + TWICE + TAIL], work[i % 2][:, IB + P:UPC],
                                  act_s[:, i % 2, P:IB], ALU.mult).then_inc(slot_hid, 1)

            def hid_split(i):
                dve.wait_ge(hidt_his, i + 1)
                if i >= 2:
                    dve.wait_ge(slot_down, i - 1)
                split_lo(hidt_lo[i % 2], acc[i % 2], hidt_hi[i % 2], hidt_los)

            dve.wait_ge(hid_los_v, len(VECTOR_LO))
            dve.memset(hid_s[:, :, IB:FB * P], 0.0).then_inc(hid_zero, 1)
            add_shared(0)
            slot_split(0)
            slot_split(1)
            add_shared(1)
            for i in range(TILES + 1):
                if i < TILES:
                    slot_hidden(i)
                if i >= 1:
                    hid_split(i - 1)
                if i + 2 < TILES:
                    slot_split(i + 2)
                if WEIGHTS_AT <= i < WEIGHTS_AT + HALVES * WEIGHT_STEPS:
                    h, step = divmod(i - WEIGHTS_AT, WEIGHT_STEPS)
                    find_weights(h, step)
            dve.wait_ge(shared_added, 2 * HALVES)
            dve.wait_ge(weight_link, HALVES * WEIGHT_STEPS)
            for b in range(2 * HALVES):
                combine(b)

        @block.tensor
        def _(pe):
            def turn(n, k, dst):
                if n >= 1:
                    pe.wait_ge(normed, TT * (n + 1))
                    pe.wait_ge(ht_los, KD * n - KD + k + 1)
                if n == 3:
                    pe.wait_ge(slots_ready if k == 0 else shifted, 1)
                for t in range(TT):
                    if n == 0:
                        pe.wait_ge(normed, t + 1)
                    src = hn[:, t, P * k:P * k + P] if n != 2 else rows[:, 0, t, P * k:P * k + P]
                    mm = pe.transpose(dst[:, P * t:P * t + P], src, ident)
                mm.then_inc(turned, 1)

            def up_passes(dst, hi, lo, s, h):
                cols = slice(TH * h, TH * h + TH)
                pe.wait_ge(ht_his, KD * (HALVES * s + h + 1))
                for k in range(KD):
                    pe.matmul(dst[:, :], hi(k), ht_hi[s][:, k, cols], start=(k == 0), stop=False)
                    pe.matmul(dst[:, :], lo(k), ht_hi[s][:, k, cols], start=False, stop=False)
                pe.wait_ge(ht_los, KD * (HALVES * s + h + 1))
                for k in range(KD):
                    mm = pe.matmul(dst[:, :], hi(k), ht_lo[s][:, k, cols], start=False, stop=(k == KD - 1))
                return mm

            def up(n):
                h, e, f = half_a(n), n % TILES_A // (FA // P), n % (FA // P)
                pe.wait_ge(c_los, e + 1)
                if n >= 2:
                    pe.wait_ge(masked, n - 1)
                up_passes(work[n % 2], lambda k: c_hi[:, e, D * k + P * f:D * k + P * f + P],
                          lambda k: c_lo[:, e, D * k + P * f:D * k + P * f + P], 0, h).then_inc(up_a, 1)

            def up_1(n):
                h, g = half_b(n), tile_b(n)
                block_split(pe, g)
                if n == B0:
                    pe.wait_ge(masked, STEPS_A)
                else:
                    pe.wait_ge(silus, n)
                up_passes(work[0], lambda k: ws_hi[:, g, P * k:P * k + P],
                          lambda k: ws_lo[:, g, P * k:P * k + P], 1, h).then_inc(up_a, 1)

            def up_3(n):
                h, g = half_b(n), tile_b(n)
                if n > B0:
                    pe.wait_ge(hiddens, n)
                up_passes(work[1], lambda k: ws_hi[:, g, P * (KD + k):P * (KD + k) + P],
                          lambda k: ws_lo[:, g, P * (KD + k):P * (KD + k) + P], 1, h).then_inc(up_b, 1)

            def down(n):
                if n < B0:
                    h, first, last = half_a(n), n % TILES_A == 0, n % TILES_A == TILES_A - 1
                    e, f = n % TILES_A // (FA // P), n % (FA // P)
                    hi, lo = c_hi[:, e, D * f:D * f + D], c_lo[:, e, D * f:D * f + D]
                else:
                    h, g = half_b(n), tile_b(n)
                    first, last = g == 0, g == SHARED_TILES - 1
                    hi, lo = ws_hi[:, g, SHARED_COLS - D:SHARED_COLS], ws_lo[:, g, SHARED_COLS - D:SHARED_COLS]
                    if first:
                        pe.wait_ge(resid, 2 * (h + 1))
                def rows_of(t):
                    return slice(P * t, P * t + P)

                def part_of(t):
                    return acc[2 * h + t // 2][:, D * (t % 2):D * (t % 2) + D]

                pe.wait_ge(hid_his, n + 1)
                for t in range(TT):
                    pe.matmul(part_of(t), h_hi[n % SPLITS][:, rows_of(t)], hi, start=(first and t % 2 == 0),
                              stop=False, skip_group_check=True)
                    pe.matmul(part_of(t), h_hi[n % SPLITS][:, rows_of(t)], lo, start=False, stop=False,
                              skip_group_check=True)
                if n == B0 + 1:
                    count(1)
                hidden_split(pe, n)
                for t in range(TT):
                    mm = pe.matmul(part_of(t), h_lo[n % SPLITS][:, rows_of(t)], hi, start=False, stop=last,
                                   skip_group_check=True)
                mm.then_inc(downs, 1)

            def gate(h):
                pe.wait_ge(g_los, 1)
                pe.wait_ge(ht_los, KD * (HALVES + h) + 1)
                for part, ready in ((ht_hi[1], ht_his), (ht_lo[1], ht_los)):
                    pe.wait_ge(ready, KD * (HALVES + h + 1))
                    for t in range(TT):
                        rows = slice(TH * h + P * t, TH * h + P * t + P)
                        for k in range(KD):
                            mm = pe.matmul(work[2][:, 2 * EB * t:2 * EB * t + 2 * EB], part[:, k, rows],
                                           g_hl[:, k, :], start=(part is ht_hi[1] and k == t == 0),
                                           stop=(part is ht_lo[1] and k == KD - 1), skip_group_check=True)
                mm.then_inc(gated, 1)

            def count(h):
                pe.wait_ge(chosens, h + 1)
                if h == 0:
                    pe.wait_ge(before_ready, 1)
                    pe.wait_ge(fills, 3)
                before = [chosen_0[:, :]] if h == 1 else []
                for t in range(TT):
                    dst = work[2][:, EB * t:EB * t + EB]
                    whole = before + [chosen[:, TT * h + u, :] for u in range(t)]
                    pe.matmul(dst, before_b[:, :], chosen[:, TT * h + t, :], start=True, stop=not whole)
                    for v in whole:
                        pe.matmul(dst, ones_b[:, :], v, start=False, stop=v is whole[-1])
                dst = work[2][:, TT * EB:TT * EB + EB]
                whole = before + [chosen[:, TT * h + u, :] for u in range(TT)]
                for v in whole:
                    mm = pe.matmul(dst, ones_b[:, :], v, start=v is whole[0], stop=v is whole[-1])
                mm.then_inc(counted, 1)

            def warm_up():
                pe.matmul(work[0][:, :], ones_b[:, :], ones_b[:, :].unsqueeze(1).broadcast_to([P, TH // P, P]),
                          start=True, stop=True)

            pe.wait_ge(fills, 1)
            for _ in range(WARM_UPS):
                warm_up()
            pe.wait_ge(cst_in, 16)
            for k in range(KD):
                turn(0, k, work[2 + k])
            for n in range(STEPS_A):
                up(n)
                if n == COUNT_A:
                    count(0)
                if n >= LAG_A:
                    down(n - LAG_A)
                for m, at in ((1, LN1B), (2, LN2A)):
                    if n == at["turn"]:
                        for k in range(KD):
                            turn(m, k, work[2 + k])
                if n == PICK_A:
                    gate(0)
            down(STEPS_A - 3)
            for n in range(B0, STEPS):
                up_1(n)
                if n == B0:
                    down(STEPS_A - 2)
                    down(STEPS_A - 1)
                if n == B0 + 2:
                    gate(1)
                up_3(n)
                if n > B0:
                    down(n - 1)
                if n == B0 + 1:
                    for k in range(KD):
                        turn(3, k, work[2 + k])
            down(STEPS - 1)
            pe.wait_ge(silus, STEPS)

            for _ in range(WARM_SLOTS):
                warm_up()
            pe.wait_ge(experts_ready, 1)
            pe.wait_ge(w_los_dve, BLOCKS - POOL_BLOCKS)
            pe.wait_ge(w_los_pool, POOL_BLOCKS)
            pe.wait_ge(hid_zero, 1)
            held = {}

            def slot_turn(i):
                pe.wait_ge(slot_ins[i % SLOT_INS], 16 * (i // SLOT_INS + 1))
                if i >= 2:
                    pe.wait_ge(slot_los, i - 1)
                for k in range(KD):
                    mm = pe.transpose(work[2 + i % 2][:, P * k:P * k + P],
                                      slot_in[i % SLOT_INS][:, P * k:P * k + P], ident)
                mm.then_inc(slot_turned, 1)

            def slot_products(i):
                pe.wait_ge(slot_his, i + 1)
                if i >= 2:
                    pe.wait_ge(slot_hid, i - 1)
                dst = work[i % 2][:, 0:UPC]

                def w(part, k):
                    return part[:, bass.ds(held[i], 1), UPC * k:UPC * k + UPC]

                for k in range(KD):
                    rows_hi = slot_hi[i % 2][:, P * k:P * k + P]
                    pe.matmul(dst, rows_hi, w(we_hi, k), start=(k == 0), stop=False)
                    pe.matmul(dst, rows_hi, w(we_lo, k), start=False, stop=False)
                pe.wait_ge(slot_los, i + 1)
                for k in range(KD):
                    mm = pe.matmul(dst, slot_lo[i % 2][:, P * k:P * k + P], w(we_hi, k), start=False,
                                   stop=(k == KD - 1))
                mm.then_inc(slot_up, 1)

            def hid_turn(i):
                pe.wait_ge(slot_hid, i + 1)
                if i < 2:
                    pe.wait_ge(shared_added, i + 1)
                else:
                    pe.wait_ge(hidt_los, i - 1)
                for k in range(FB):
                    mm = pe.transpose(acc[i % 2][:, P * k:P * k + P], hid_s[:, i % 2, P * k:P * k + P], ident)
                mm.then_inc(hid_turned, 1)

            def slot_results(i):
                pe.wait_ge(hidt_his, i + 1)
                if i < 2:
                    pe.wait_ge(shared_added, 2 + i + 1)
                else:
                    pe.wait_ge(slot_done, i - 1)
                e = held.pop(i)
                dst, hi, lo = acc[2 + i % 2][:, 0:D], hidt_hi[i % 2], hidt_lo[i % 2]

                def w(part, k, rows=P):
                    return part[0:rows, bass.ds(e, 1), KD * UPC + D * k:KD * UPC + D * k + D]

                pe.matmul(dst, hi[:, 0:P], w(we_hi, 0), start=True, stop=False)
                pe.matmul(dst, hi[:, 0:P], w(we_lo, 0), start=False, stop=False)
                pe.matmul(dst, hi[:, P:2 * P], w(we_hi, 1), start=False, stop=False)
                pe.wait_ge(hidt_los, i + 1)
                pe.matmul(dst, lo[:, 0:P], w(we_hi, 0), start=False, stop=False)
                pe.matmul(dst, lo[0:TWICE, P:2 * P], w(we_hi, 1, TWICE), start=False,
                          stop=True).then_inc(slot_down, 1)

            def hold_expert(i):
                held[i] = pe.value_load(expert[0:1, i:i + 1], min_val=0, max_val=EB - 1)

            for i in range(2):
                hold_expert(i)
            slot_turn(0)
            slot_turn(1)
            for i in range(TILES + 2):
                if i < TILES:
                    slot_products(i)
                if i + 2 < TILES:
                    hold_expert(i + 2)
                if 1 <= i < TILES + 1:
                    hid_turn(i - 1)
                if i + 2 < TILES:
                    slot_turn(i + 2)
                if i >= 2:
                    slot_results(i - 2)


def kernel(**inputs):
    import numpy as np
    import concourse.bacc as bacc
    from concourse.bass_utils import run_bass_kernel_spmd as run

    x = np.asarray(inputs["x"])
    tok = np.ascontiguousarray(np.asarray(inputs["itok_BxS_13_99985"]).reshape(T))
    c = np.asarray(inputs["ctx_2048"])

    def by_slices(m, slices):
        *lead, rows, n = m.shape
        return m.reshape(*lead, slices, P, n).swapaxes(-3, -2).reshape(*lead, P, slices * n)

    def padded(m, rows):
        out = np.zeros((*m.shape[:-2], rows, m.shape[-1]), m.dtype)
        out[..., :m.shape[-2], :] = m
        return out

    ctx_t = np.ascontiguousarray(by_slices(c.transpose(0, 2, 1), KD))
    a = {k: np.asarray(inputs["L0_ffn_" + k]) for k in ("gate_w", "w1", "w2", "w3", "sw1", "sw2", "sw3")}
    up_1, up_3 = (by_slices(padded(a[k], SHARED_TILES * P).reshape(SHARED_TILES, P, D).transpose(0, 2, 1), KD)
                  for k in ("sw1", "sw3"))
    down = padded(a["sw2"].T, SHARED_TILES * P).reshape(SHARED_TILES, P, D)
    w_shared = np.ascontiguousarray(np.concatenate([up_1, up_3, down], axis=2))
    up_13 = by_slices(np.concatenate([a["w1"].transpose(0, 2, 1), a["w3"].transpose(0, 2, 1)], axis=2), KD)
    down = a["w2"].transpose(0, 2, 1)
    down = padded(np.concatenate([padded(down, P + TWICE), down[:, P:]], axis=1), FB * P)
    down = by_slices(down, FB)
    w_expert = np.ascontiguousarray(np.concatenate([up_13, down], axis=2))
    gate_t = np.ascontiguousarray(by_slices(a["gate_w"].T, KD).reshape(P, KD, EB))

    def on_all(row):
        return np.tile(np.asarray(row, np.float32).reshape(1, -1), (P, 1))

    token = np.arange(T).reshape(HALVES * TT, P)
    consts = np.ascontiguousarray(np.concatenate([
        np.eye(P, dtype=np.float32),
        np.triu(np.ones((P, P), np.float32), 1),
        on_all(np.tile(np.arange(EB), TT)),
        on_all(np.tile(P * np.arange(EB), EB)),
        on_all(np.tril(np.ones((EB, EB)), -1)),
        on_all(np.arange(TILES)),
        np.concatenate([token, token + T]).T.astype(np.float32)], axis=1))

    nc = bacc.Bacc("TRN2", target_bir_lowering=False, num_devices=1)
    arrays, args = {}, []
    for name, v in (("x", np.ascontiguousarray(x.reshape(T, D))), ("tok", tok), ("ctx_t", ctx_t),
                    ("gate_t", gate_t), ("w_shared", w_shared), ("w_expert", w_expert), ("consts", consts)):
        arrays[name] = v
        args.append(nc.dram_tensor(name, v.shape, mybir.dt.from_np(v.dtype), kind="ExternalInput").ap())
    args.append(nc.dram_tensor("slot_rows", (TILES * P, ROW), F32, kind="Internal").ap())
    args.append(nc.dram_tensor("result_rows", (TOP * T, D), F32, kind="Internal").ap())
    args.append(nc.dram_tensor("out", (T, D), F32, kind="ExternalOutput").ap())
    build(nc, *args)
    r = run(nc, [arrays], core_ids=[0])
    return r.results[0]["out"].reshape(x.shape)
```
